# Optimizing a Trainium2 kernel written in Bass

```python
import numpy as np
import jax
import jax.numpy as jnp

def _softmax(x, axis=-1):
    return jax.nn.softmax(x, axis=axis)

def _gelu(x):
    return jax.nn.gelu(x, approximate=True)

def _silu(x):
    return jax.nn.silu(x)

def _sigmoid(x):
    return jax.nn.sigmoid(x)

def _layernorm(x, axis=-1, eps=1e-05):
    m = jnp.mean(x, axis=axis, keepdims=True)
    v = jnp.var(x, axis=axis, keepdims=True)
    return (x - m) / jnp.sqrt(v + eps)

def _scatter_add(tgt, idx, src, axis=0):
    return tgt.at[idx].add(src)

def _segment_sum(src, seg, n):
    return jax.ops.segment_sum(src, seg, n)
kernel_name = 'mk_adj_ffn_d1_adj_r2_f7653c'

def setup_inputs(seed: int=0):
    np.random.seed(seed)
    _w = jnp.asarray

    def _rec_inputs():
        import jax
        import jax.numpy as jnp
        _gk = jax.random.key(seed)
        x = -0.0005146 + 1 * jax.random.normal(jax.random.fold_in(_gk, 1), (8, 1024, 128), jnp.float32)
        _a = jax.random.bernoulli(jax.random.fold_in(_gk, 2), 0.015625, (8, 1024, 1024))
        _a = jnp.logical_or(_a, jnp.swapaxes(_a, -1, -2))
        _a = jnp.logical_or(_a, jnp.eye(1024, dtype=bool))
        adj = _a.astype(jnp.int32)
        return (x, adj)
    x, adj = _rec_inputs()

    def _L0_gnn_setup():
        import jax, jax.numpy as jnp
        import numpy as np
        B, N, C, OUT, S = (4, 1024, 128, 128, 25)
        DENSITY = 0.008
        key = jax.random.key(seed)
        kA, kX, kW = jax.random.split(key, 3)
        A = jax.random.bernoulli(kA, DENSITY, (B, N, N)).astype(jnp.int32)
        X = jax.random.normal(kX, (B, N, C), dtype=jnp.float32)
        W = jax.random.normal(kW, (2 * C, OUT), dtype=jnp.float32) * np.float32(1.0 / np.sqrt(2 * C))
        b = jnp.zeros((OUT,), dtype=jnp.float32)
        return {'A': A, 'X': X, 'W': W, 'b': b}
    _L0_gnn_all = _L0_gnn_setup()
    _L0_gnn_in = {k: v for k, v in _L0_gnn_all.items() if k in ('W', 'b')}
    del _L0_gnn_all

    def _L0_ffn_setup():
        import jax, jax.numpy as jnp
        import numpy as np
        D_MODEL = 128
        N_EXPERTS = 16
        HIDDEN = 256
        SCALE = 0.02
        key = jax.random.key(seed)
        ks = jax.random.split(key, 5)
        x = jax.random.normal(ks[0], (4, 4096, D_MODEL), dtype=jnp.float32)
        gate_w = jax.random.normal(ks[1], (D_MODEL, N_EXPERTS), dtype=jnp.float32) * SCALE
        gate_b = jnp.zeros((N_EXPERTS,), dtype=jnp.float32)
        w1 = jax.random.normal(ks[2], (N_EXPERTS, D_MODEL, HIDDEN), dtype=jnp.float32) * SCALE
        w2 = jax.random.normal(ks[3], (N_EXPERTS, D_MODEL, HIDDEN), dtype=jnp.float32) * SCALE
        w3 = jax.random.normal(ks[4], (N_EXPERTS, HIDDEN, D_MODEL), dtype=jnp.float32) * SCALE
        return {'x': x, 'gate_w': gate_w, 'gate_b': gate_b, 'w1': w1, 'w2': w2, 'w3': w3}
    _L0_ffn_all = _L0_ffn_setup()
    _L0_ffn_in = {k: v for k, v in _L0_ffn_all.items() if k in ('gate_w', 'gate_b', 'w1', 'w2', 'w3')}
    del _L0_ffn_all
    return {'x': x, 'adj': adj, 'L0_gnn_W': _L0_gnn_in['W'], 'L0_gnn_b': _L0_gnn_in['b'], 'L0_ffn_gate_w': _L0_ffn_in['gate_w'], 'L0_ffn_gate_b': _L0_ffn_in['gate_b'], 'L0_ffn_w1': _L0_ffn_in['w1'], 'L0_ffn_w2': _L0_ffn_in['w2'], 'L0_ffn_w3': _L0_ffn_in['w3']}

def reference(x, adj, L0_gnn_W, L0_gnn_b, L0_ffn_gate_w, L0_ffn_gate_b, L0_ffn_w1, L0_ffn_w2, L0_ffn_w3):
    import jax
    import jax.numpy as jnp

    def _L0_gnn_ref(A, X, W, b):
        import jax, jax.numpy as jnp
        import numpy as np
        B, N, C, OUT, S = (4, 1024, 128, 128, 25)
        DENSITY = 0.008
        mask = A != 0
        neg_inf = jnp.float32(-jnp.inf)
        pri = -jnp.arange(N, dtype=jnp.float32)
        scores = jnp.where(mask, pri, neg_inf)
        vals, idx = jax.lax.top_k(scores, S)
        valid = vals > neg_inf
        feats = jax.vmap(lambda x, i: x[i])(X, idx)
        feats = jnp.where(valid[..., None], feats, neg_inf)
        agg = feats.max(axis=2)
        degree = mask.sum(axis=-1)
        agg = jnp.where((degree <= S)[..., None], jnp.maximum(agg, 0.0), agg)
        h = jnp.concatenate([X, agg], axis=-1)
        out = jax.nn.relu(jnp.einsum('bnf,fo->bno', h, W) + b)
        return out

    def _L0_ffn_ref(x, gate_w, gate_b, w1, w2, w3):
        import jax, jax.numpy as jnp
        import numpy as np
        D_MODEL = 128
        N_EXPERTS = 16
        HIDDEN = 256
        SCALE = 0.02
        n_experts = w1.shape[0]
        logits = jnp.einsum('bsd,de->bse', x, gate_w) + gate_b
        probs = jax.nn.softmax(logits, axis=-1)
        top_probs, top_idx = jax.lax.top_k(probs, 2)
        top_probs = top_probs / jnp.sum(top_probs, axis=-1, keepdims=True)
        dispatch = jnp.sum(jax.nn.one_hot(top_idx, n_experts, dtype=x.dtype) * top_probs[..., None], axis=-2)
        h1 = jnp.einsum('bsd,edh->bseh', x, w1)
        h2 = jnp.einsum('bsd,edh->bseh', x, w2)
        hidden = jax.nn.silu(h1) * h2
        expert_out = jnp.einsum('bseh,eho->bseo', hidden, w3)
        return jnp.einsum('bseo,bse->bso', expert_out, dispatch)
    x = x + _L0_gnn_ref(adj, _layernorm(x, axis=-1), L0_gnn_W, L0_gnn_b)
    x = x + _L0_ffn_ref(_layernorm(x, axis=-1), L0_ffn_gate_w, L0_ffn_gate_b, L0_ffn_w1, L0_ffn_w2, L0_ffn_w3)
    return x

_drawn_inputs = setup_inputs


def setup_inputs(seed=0):
    import zlib

    import numpy as np

    out = dict(_drawn_inputs(seed))
    spreads = {'L0_gnn_b': (0.0, 0.1), 'L0_ffn_gate_b': (0.0, 0.8)}
    factors = {'L0_ffn_gate_w': 8.0, 'L0_ffn_w1': 8.0, 'L0_ffn_w2': 8.0, 'L0_ffn_w3': 8.0}
    for name, (base, spread) in spreads.items():
        noise = np.random.default_rng([zlib.crc32(name.encode()), seed]).standard_normal(out[name].shape)
        drawn = base * np.exp(spread * noise) if base else spread * noise
        out[name] = jnp.asarray(drawn.astype(out[name].dtype))
    for name, factor in factors.items():
        out[name] = (out[name] * factor).astype(out[name].dtype)
    return out
```

```python
import concourse.bass as bass
from concourse import mybir
from contextlib import ExitStack
import numpy as np


def build(nc, x, adj, W, bias, gate_w, gate_b, w1, w2, w3, out):
    f32, f16, i32, u32 = mybir.dt.float32, mybir.dt.float16, mybir.dt.int32, mybir.dt.uint32
    ALU = mybir.AluOpType
    ACT = mybir.ActivationFunctionType
    AX = mybir.AxisListType
    ds = bass.ds

    P = 128
    B, N, C = x.shape
    NE, _, HID = w1.shape
    NB = N // P
    CH = 512
    CT = CH // P
    HALVES = N // CH
    NCHUNK = B * HALVES
    TILES = B * NB
    S = 25
    SHIFT = 64
    PIECE = 2
    NPIECE = NB // PIECE
    NRING = 5
    EPS = 1e-5
    SCALE = 4096.0
    assert SCALE * np.sqrt(C - 1) < 65504 and S % NRING == 0 and S < SHIFT and HALVES == 2
    BIG = 3.0e38
    PAIR_TILES = TILES * P * 2 // P + NE
    assert PAIR_TILES % 4 == 0

    x_rows = x.rearrange("b n c -> (b n) c")
    adj_rows = adj.rearrange("b n m -> (b n) m")
    out_rows = out.rearrange("b n c -> (b n) c")
    dispatched = nc.dram_tensor("dispatched", (PAIR_TILES * P, C), f32).ap()
    expert_rows = nc.dram_tensor("expert_rows", (PAIR_TILES * P, C), f32).ap()

    ctx = ExitStack()
    with ctx:
        def sb(name, shape, dt):
            return ctx.enter_context(nc.sbuf_tensor(name, shape, dt))

        def sem(name):
            return ctx.enter_context(nc.semaphore(name))

        x1 = sb("x1", [P, TILES, C], f32)
        x2n = sb("x2n", [P, TILES, C], f32)
        adj_in = sb("adj_in", [P, CT, N], i32)
        mask_nm = sb("mask_nm", [P, CT, N], f16)
        mask_t = sb("mask_t", [P, NB, CH], f16)
        rank_t = sb("rank_t", [P, 2, NB, CH], f16)
        onehot = sb("onehot", [P, NRING, NB * CH], f16)
        xparts = sb("xparts", [P, 2, NB, 2, C], f16)
        xin = sb("xin", [P, 2, NB, C], f32)
        xs = sb("xs", [P, 2, NB, C], f32)
        agg = sb("agg", [P, 2, CH], f32)
        xs_t = sb("xs_t", [P, CH], f32)
        gnn_tmp = sb("gnn_tmp", [P, CT, C], f32)
        x2_cur = sb("x2_cur", [P, CT, C], f32)
        x2_t = sb("x2_t", [P, CH], f32)
        logits = sb("logits", [P, TILES, NE], f32)
        stats1 = sb("stats1", [P, NB, 6], f32)
        mv1 = sb("mv1", [P, NB, 2], f32)
        std1 = sb("std1", [P, 3, NB], f32)
        stats2 = sb("stats2", [P, CT, 6], f32)
        mv2 = sb("mv2", [P, CT, 2], f32)
        std2 = sb("std2", [P, 3, CT], f32)
        w_gnn = sb("w_gnn", [P, 2, C], f32)
        bias_bc = sb("bias_bc", [P, C], f32)
        gw = sb("gw", [P, NE], f32)
        gb_bc = sb("gb_bc", [P, NE], f32)
        ident16 = sb("ident16", [P, P], f16)
        ident32 = sb("ident32", [P, P], f32)
        rank_mat = sb("rank_mat", [P, P], f16)
        tri = sb("tri", [P, P], f16)
        ones = sb("ones", [P, P], f16)
        w12 = onehot[:, 0:4, :].rearrange("p r f -> p (r f)").bitcast(f32).rearrange("p (e h) -> p e h", e=NE)
        w3_sb = adj_in[:, :, :].rearrange("p t n -> p (t n)").bitcast(f32).rearrange("p (e k o) -> p e k o", e=NE, k=2)
        rt = rank_t[:, :, :, :].rearrange("p a b c -> p (a b c)").bitcast(f32)
        assert rank_t.shape[1] * NB * CH // 2 >= 4 * TILES * NE
        RN = TILES * NE

        def words(tensor, i):
            return tensor[:, i * RN:(i + 1) * RN].rearrange("p (t e) -> p t e", e=NE)

        oh1, oh2, lmask, pos_e = (words(rt, i) for i in range(4))
        mt = mask_t[:, :, :].rearrange("p a b -> p (a b)").bitcast(f32)
        eqi, tile_inc = (words(mt, i) for i in range(2))
        xi = xin[:, :, :, :].rearrange("p a b c -> p (a b c)")
        tile_tot, in_tile = (words(xi, i) for i in range(2))
        sel16 = xparts[:, 0, :, :, :].rearrange("p a b c -> p (a b c)")[:, 0:RN]
        iota_m = sb("iota_m", [P, NE], f32)
        iota_j = sb("iota_j", [P, PAIR_TILES], f32)
        small = sb("small", [P, 12, TILES], f32)
        cnt = sb("cnt", [P, 6, NE], f32)
        cnt_i = sb("cnt_i", [P, 2, NE], i32)
        cmp_j = xs[:, :, :, :].rearrange("p a b c -> p (a b c)")
        expert_f = sb("expert_f", [P, PAIR_TILES], f32)
        expert_i = sb("expert_i", [P, PAIR_TILES], i32)
        pos_i = sb("pos_i", [P, 2, TILES], i32)
        weight = sb("weight", [P, 2, TILES], f32)
        XB = 4
        mk = mask_nm[:, :, :].rearrange("p a b -> p (a b)").bitcast(f32)
        xd = mk[:, 0:XB * P].rearrange("p (r c) -> p r c", r=XB)
        yd = mk[:, XB * P:2 * XB * P].rearrange("p (r c) -> p r c", r=XB)
        zero = sb("zero", [P, 512], f32)
        silu, hid, hid_t = (mt[:, i * 2 * HID:(i + 1) * 2 * HID].rearrange("p (r h) -> p r h", r=2) for i in range(3))
        xd_t = mt[:, 6 * HID:6 * HID + 2 * P].rearrange("p (r c) -> p r c", r=2)
        GB = 4
        yg = x2n[:, 0:2 * GB, :]
        res = x2n[:, 2 * GB:3 * GB, :]
        res_t = x2n[:, 3 * GB:4 * GB, :]

        bank = [ctx.enter_context(nc.psum_tensor(f"slot{i}", [P, CH], f32)) for i in range(NRING)]
        tr_ps = ctx.enter_context(nc.psum_tensor("tr_ps", [P, PIECE, CH], f16))
        rk_ps = ctx.enter_context(nc.psum_tensor("rk_ps", [P, CH], f32))
        fin_ps = ctx.enter_context(nc.psum_tensor("fin_ps", [P, CH], f32))

        s_w = sem("weights_loaded")
        s_const = sem("constants_ready")
        s_zero = sem("zero_ready")
        s_zeroed = sem("dispatch_zeroed")
        s_adj = [sem(f"adj_loaded{i}") for i in range(CT)]
        s_x = [sem(f"x_loaded{i}") for i in range(2)]
        s_mask = sem("mask_done")
        s_tr = sem("mask_transposed")
        s_tev = sem("mask_t_done")
        s_rk = sem("rank_product_done")
        s_rev = sem("rank_t_done")
        s_init = sem("agg_started")
        s_oh = sem("onehot_done")
        s_slot = sem("slot_product_done")
        s_max = sem("max_done")
        s_ln1 = sem("ln1_chain")
        s_std1 = sem("std1_done")
        s_hi = sem("hi_part_done")
        s_parts = sem("x_parts_done")
        s_xt = sem("xs_transposed")
        s_xtev = sem("xs_t_done")
        s_fin = sem("gnn_product_done")
        s_tmp = sem("gnn_tmp_done")
        s_x1 = sem("x1_done")
        s_ln2 = sem("ln2_chain")
        s_std2 = sem("std2_done")
        s_x2 = sem("x2_cur_done")
        s_x2c = sem("x2n_kept")
        s_x2t = sem("x2_transposed")
        s_x2tev = sem("x2_t_done")
        s_lg = sem("logit_product_done")
        s_lgd = sem("logits_done")
        s_rc = sem("routing_chain")
        s_sel = sem("sel_ready")
        s_cntp = sem("counts_product_done")
        s_diff = sem("logit_gap_ready")
        s_exp = sem("exp_done")
        s_pos = sem("positions_ready")
        s_wexp = sem("expert_weights_loaded")
        s_scat = sem("scattered")
        s_xd = [sem(f"rows_loaded{i}") for i in range(4)]
        s_xdt = sem("rows_transposed")
        s_xdtev = sem("rows_t_done")
        s_h = sem("hidden_product_done")
        s_silu = sem("silu_done")
        s_hid = sem("hidden_done")
        s_ht = sem("hidden_transposed")
        s_htev = sem("hidden_t_done")
        s_y = sem("expert_product_done")
        s_yev = sem("expert_row_ready")
        s_yst = [sem(f"expert_rows_stored{i}") for i in range(4)]
        s_g = [sem(f"gathered{i}") for i in range(4)]
        s_c1 = sem("combine_first")
        s_c2 = sem("combine_second")
        s_res = sem("result_ready")
        s_out = [sem(f"out_stored{i}") for i in range(4)]

        def wait(eng, s, value):
            if not (isinstance(value, int) and value <= 0):
                eng.wait_ge(s, value)

        def chunks(eng, slots):
            slots(0, 0, 0, True, False)
            with eng.Fori(0, B - 1) as b:
                slots(2 * b + 1, b, 1, True, True)
                slots(2 * b + 2, b + 1, 0, True, True)
            slots(NCHUNK - 1, B - 1, 1, False, True)

        N_CONST = 12
        LN1_VAR, LN1 = 3, 5
        LN2_VAR, LN2 = 3, 4

        block = ctx.enter_context(nc.Block())

        @block.sync
        def _(sp):
            def load_x(k, b, h):
                wait(sp, s_x1, k - 1)
                sp.dma_start(xin[:, h, :, :], x_rows[ds(b * N, N), :].rearrange("(t p) c -> p t c", p=P))\
                    .then_inc(s_x[h], 16)

            def load_adj(k, i):
                wait(sp, s_mask, CT * (k - 1) + i + 1)
                sp.dma_start(adj_in[:, i, :], adj_rows[ds(k * CH + i * P, P), :]).then_inc(s_adj[i], 16)

            load_x(0, 0, 0)
            for i in range(CT):
                load_adj(0, i)
            sp.dma_start(w_gnn[:, :, :], W.rearrange("(k p) o -> p k o", p=P)).then_inc(s_w, 16)
            sp.dma_start(bias_bc[:, :], bias.rearrange("(a o) -> a o", a=1).broadcast_to([P, C])).then_inc(s_w, 16)
            sp.dma_start(gw[:, :], gate_w).then_inc(s_w, 16)
            sp.dma_start(gb_bc[:, :], gate_b.rearrange("(a o) -> a o", a=1).broadcast_to([P, NE])).then_inc(s_w, 16)
            load_x(1, 0, 1)
            for i in range(CT):
                load_adj(1, i)
            sp.wait_ge(s_zero, 1)
            for i in range(PAIR_TILES // 4):
                sp.dma_start(dispatched[i * 4 * P:(i + 1) * 4 * P, :].rearrange("(p r) c -> p (r c)", p=P),
                             zero[:, :]).then_inc(s_zeroed, 16)
            with sp.Fori(0, B - 1) as b:
                for i in range(CT):
                    load_adj(2 * b + 2, i)
                load_x(2 * b + 2, b + 1, 0)
                for i in range(CT):
                    load_adj(2 * b + 3, i)
                load_x(2 * b + 3, b + 1, 1)

            sp.wait_ge(s_slot, S * NCHUNK)
            sp.wait_ge(s_mask, CT * NCHUNK)
            sp.dma_start(w12[:, :, 0:HID], w1.rearrange("e d h -> d e h")).then_inc(s_wexp, 16)
            sp.dma_start(w12[:, :, HID:2 * HID], w2.rearrange("e d h -> d e h")).then_inc(s_wexp, 16)
            for k in range(2):
                sp.dma_start(w3_sb[:, :, k, :], w3[:, k * P:(k + 1) * P, :].rearrange("e h o -> h e o"))\
                    .then_inc(s_wexp, 16)

            def load_rows(j, u):
                wait(sp, s_xdt, j - 3)
                sp.dma_start(xd[:, u, :], dispatched[ds(j * P, P), :]).then_inc(s_xd[u], 16)

            def store_rows(j, u):
                sp.wait_ge(s_yev, j + 1)
                sp.dma_start(expert_rows[ds(j * P, P), :], yd[:, u, :]).then_inc(s_yst[u], 16)

            sp.wait_ge(s_scat, 2 * TILES * 16)
            sp.wait_ge(s_zeroed, (PAIR_TILES // 4) * 16)
            for u in range(4):
                load_rows(u, u)
            with sp.Fori(0, PAIR_TILES // 4 - 1) as i:
                for u in range(4):
                    store_rows(4 * i + u, u)
                    load_rows(4 * i + 4 + u, u)
            for u in range(4):
                store_rows(PAIR_TILES - 4 + u, u)

            for t in range(TILES):
                sp.wait_ge(s_res, t + 1)
                sp.dma_start(out_rows[t * P:(t + 1) * P, :], res[:, t % GB, :]).then_inc(s_out[t % GB], 16)
            for g in range(GB):
                sp.wait_ge(s_out[g], 16 * TILES // GB)

        @block.gpsimd
        def _(pool):
            pool.sem_inc(s_x2c, 1)
            n = [0]

            def done(ins):
                n[0] += 1
                ins.then_inc(s_const, 1)

            pool.memset(zero[:, :], 0.0).then_inc(s_zero, 1)
            done(pool.memset(ident16[:, :], 0.0))
            done(pool.memset(ident32[:, :], 0.0))
            done(pool.memset(rank_mat[:, :], 1.0))
            done(pool.memset(tri[:, :], 1.0))
            done(pool.memset(ones[:, :], 1.0))
            pool.wait_ge(s_const, n[0])
            for m in (ident16, ident32):
                done(pool.affine_select(out=m[:, :], in_=m[:, :], compare_op=ALU.not_equal, fill=1.0, base=0,
                                        pattern=[[-1, P]], channel_multiplier=1))
            for m in (rank_mat, tri):
                done(pool.affine_select(out=m[:, :], in_=m[:, :], compare_op=ALU.is_gt, fill=0.0, base=0,
                                        pattern=[[1, P]], channel_multiplier=-1))
            pool.wait_ge(s_const, n[0])
            done(pool.affine_select(out=rank_mat[:, :], in_=rank_mat[:, :], compare_op=ALU.not_equal,
                                    fill=-float(SHIFT), base=0, pattern=[[-1, P]], channel_multiplier=1))
            done(pool.iota(iota_m[:, :], pattern=[[1, NE]], base=-64, channel_multiplier=0,
                           allow_small_or_imprecise_dtypes=True))
            done(pool.iota(iota_j[:, :], pattern=[[1, PAIR_TILES]], base=0, channel_multiplier=0,
                           allow_small_or_imprecise_dtypes=True))
            assert n[0] == N_CONST

            def keep_x2(k):
                pool.wait_ge(s_x2, k + 1)
                pool.nop(nofuse=True)
                pool.tensor_copy(x2n[:, ds(CT * k, CT), :], x2_cur[:, :, :]).then_inc(s_x2c, 1)

            with pool.Fori(0, NCHUNK) as k:
                keep_x2(k)

            pool.wait_ge(s_x2c, NCHUNK + 1)
            pool.wait_ge(s_zeroed, (PAIR_TILES // 4) * 16)
            pool.wait_ge(s_pos, 1)
            for t in range(TILES):
                for c in range(2):
                    pool.indirect_dma_start(
                        out=dispatched[:, :], out_offset=bass.IndirectOffsetOnAxis(ap=pos_i[:, c, t:t + 1].bitcast(u32), axis=0),
                        in_=x2n[:, t, :], in_offset=None).then_inc(s_scat, 16)

            for u in range(4):
                pool.wait_ge(s_yst[u], 16 * PAIR_TILES // 4)
            pool.wait_ge(s_scat, 2 * TILES * 16)
            for t in range(TILES):
                g = t % GB
                wait(pool, s_res, t - GB + 1)
                for c in range(2):
                    pool.indirect_dma_start(
                        out=yg[:, 2 * g + c, :], out_offset=None, in_=expert_rows[:, :],
                        in_offset=bass.IndirectOffsetOnAxis(ap=pos_i[:, c, t:t + 1].bitcast(u32), axis=0))\
                        .then_inc(s_g[g], 16)

        @block.scalar
        def _(act):
            def evac_mask(k, q):
                act.wait_ge(s_tr, NPIECE * k + q + 1)
                if q == 0:
                    wait(act, s_rk, (NB + 1) * k)
                act.activation(mask_t[:, PIECE * q:PIECE * (q + 1), :], tr_ps[:, :, :], ACT.Copy).then_inc(s_tev, 1)

            def evac_rank(k, h, j):
                act.wait_ge(s_rk, (NB + 1) * k + j + 1)
                if j == 0:
                    wait(act, s_oh, S * (k - 1))
                act.activation(rank_t[:, h, j, :], rk_ps[:, :], ACT.Copy).then_inc(s_rev, 1)

            def root1(k):
                act.wait_ge(s_ln1, LN1 * k + LN1_VAR)
                act.activation(std1[:, 1, :], std1[:, 0, :], ACT.Sqrt).then_inc(s_std1, 1)

            def hi_part(k, h):
                act.wait_ge(s_ln1, LN1 * (k + 1))
                wait(act, s_slot, S * (k - 1))
                act.activation(xparts[:, h, :, 0, :], xs[:, h, :, :], ACT.Copy).then_inc(s_hi, 1)

            def evac_xs(k):
                act.wait_ge(s_xt, k + 1)
                act.activation(xs_t[:, :], fin_ps[:, :], ACT.Copy).then_inc(s_xtev, 1)

            def root2(k):
                act.wait_ge(s_ln2, LN2 * k + LN2_VAR)
                act.activation(std2[:, 1, :], std2[:, 0, :], ACT.Sqrt).then_inc(s_std2, 1)

            def evac_x2(k):
                act.wait_ge(s_x2t, k + 2)
                act.activation(x2_t[:, :], fin_ps[:, :], ACT.Copy).then_inc(s_x2tev, 1)

            def slots(k, b, h, prep, fin):
                for s in range(S):
                    if prep and s % 2 == 1 and 3 <= s < 3 + 2 * NPIECE:
                        evac_mask(k + 1, (s - 3) // 2)
                    if fin and s == 2:
                        evac_xs(k - 1)
                    if prep and s == 9:
                        root1(k + 1)
                    if prep and s == 12:
                        hi_part(k + 1, 1 - h)
                    if fin and s == 6:
                        root2(k - 1)
                    if fin and s == 9:
                        evac_x2(k - 1)
                    if prep and 11 <= s < 11 + NB:
                        evac_rank(k + 1, 1 - h, s - 11)

            root1(0)
            hi_part(0, 0)
            for q in range(NPIECE):
                evac_mask(0, q)
            for j in range(NB):
                evac_rank(0, 0, j)
            chunks(act, slots)
            evac_xs(NCHUNK - 1)
            root2(NCHUNK - 1)
            evac_x2(NCHUNK - 1)

            act.wait_ge(s_diff, 1)
            act.activation(small[:, 3, :], small[:, 2, :], ACT.Exp).then_inc(s_exp, 1)

            def evac_rows(j, u):
                act.wait_ge(s_xdt, j + 1)
                act.activation(xd_t[:, u % 2, :], bank[u % 2][:, 0:P], ACT.Copy).then_inc(s_xdtev, 1)

            def do_silu(j, u):
                act.wait_ge(s_h, j + 1)
                wait(act, s_hid, j - 1)
                act.activation(silu[:, u % 2, :], bank[2 + u % 2][:, 0:HID], ACT.Silu).then_inc(s_silu, 1)

            def expert_tile(j, u, turn):
                if not (isinstance(j, int) and j + 1 >= PAIR_TILES):
                    do_silu(j + 1, (u + 1) % 4)
                if not (isinstance(j, int) and j + 2 >= PAIR_TILES):
                    evac_rows(j + 2, (u + 2) % 4)
                act.wait_ge(s_y, j + 1)
                wait(act, s_yst[u], 16 * turn)
                act.activation(yd[:, u, :], (rk_ps, fin_ps)[u % 2][:, 0:P], ACT.Copy).then_inc(s_yev, 1)

            evac_rows(0, 0)
            evac_rows(1, 1)
            do_silu(0, 0)
            for u in range(4):
                expert_tile(u, u, 0)
            with act.Fori(1, PAIR_TILES // 4 - 1) as i:
                for u in range(4):
                    expert_tile(4 * i + u, u, i)
            for u in range(4):
                expert_tile(PAIR_TILES - 4 + u, u, PAIR_TILES // 4 - 1)

        @block.vector
        def _(dve):
            def mask(k, i):
                dve.wait_ge(s_adj[i], 16 * (k + 1))
                if i == 0:
                    wait(dve, s_tr, NPIECE * k)
                dve.tensor_scalar(mask_nm[:, i, :], adj_in[:, i, :], 0.0, None, ALU.not_equal).then_inc(s_mask, 1)

            def ln1_stats(k, b, h):
                dve.wait_ge(s_x[h], 16 * (b + 1))
                for t in range(NB):
                    last = dve.bn_stats(stats1[:, t, :], xin[:, h, t, :])
                last.then_inc(s_ln1, 1)
                dve.wait_ge(s_ln1, LN1 * k + 1)
                dve.nop(nofuse=True)
                for t in range(NB):
                    last = dve.bn_aggr(mv1[:, t, :], stats1[:, t, :])
                last.then_inc(s_ln1, 1)
                dve.wait_ge(s_ln1, LN1 * k + 2)
                dve.tensor_scalar(std1[:, 0, :], mv1[:, :, 1], EPS, 1.0 / (SCALE * SCALE), ALU.add, ALU.mult)\
                    .then_inc(s_ln1, 1)

            def ln1_apply(k, h):
                dve.wait_ge(s_std1, k + 1)
                dve.reciprocal(std1[:, 2, :], std1[:, 1, :]).then_inc(s_ln1, 1)
                dve.wait_ge(s_ln1, LN1 * k + LN1_VAR + 1)
                wait(dve, s_xt, k - 1)
                for t in range(NB):
                    last = dve.tensor_scalar(xs[:, h, t, :], xin[:, h, t, :], mv1[:, t, 0:1], std1[:, 2, t:t + 1],
                                             ALU.subtract, ALU.mult)
                last.then_inc(s_ln1, 1)

            def lo_part(k, h):
                dve.wait_ge(s_hi, k + 1)
                dve.tensor_tensor(xparts[:, h, :, 1, :], xs[:, h, :, :], xparts[:, h, :, 0, :], ALU.subtract)\
                    .then_inc(s_parts, 1)

            def agg_init(k, h):
                dve.wait_ge(s_rk, (NB + 1) * (k + 1))
                wait(dve, s_fin, k - 1)
                dve.tensor_scalar(agg[:, h, :], rk_ps[:, :], S + 0.5, -BIG, ALU.is_gt, ALU.mult).then_inc(s_init, 1)

            def make_onehot(k, h, s):
                if s == 0:
                    dve.wait_ge(s_rev, NB * (k + 1))
                wait(dve, s_slot, S * k + s - NRING + 1)
                dve.tensor_scalar(onehot[:, s % NRING, :], rank_t[:, h, :, :].rearrange("p a b -> p (a b)"),
                                  float(s - SHIFT), None, ALU.is_equal).then_inc(s_oh, 1)

            def take_max(k, h, s):
                if s == 0:
                    dve.wait_ge(s_init, k + 1)
                dve.wait_ge(s_slot, S * k + s + 1)
                wait(dve, s_max, S * k + s)
                dve.tensor_tensor(agg[:, h, :], bank[s % NRING][:, :], agg[:, h, :], ALU.max).then_inc(s_max, 1)

            def gnn_out(k, h):
                dve.wait_ge(s_fin, k + 1)
                dve.scalar_tensor_tensor(out=gnn_tmp[:, :, :], in0=fin_ps[:, :].rearrange("p (t c) -> p t c", t=CT),
                                         scalar=1.0 / SCALE, in1=bias_bc[:, :].unsqueeze(1).broadcast_to([P, CT, C]),
                                         op0=ALU.mult, op1=ALU.add).then_inc(s_tmp, 1)
                dve.wait_ge(s_tmp, k + 1)
                dve.scalar_tensor_tensor(out=x1[:, ds(CT * k, CT), :], in0=gnn_tmp[:, :, :], scalar=0.0,
                                         in1=xin[:, h, CT * h:CT * h + CT, :], op0=ALU.max, op1=ALU.add)\
                    .then_inc(s_x1, 1)

            def ln2_stats(k):
                dve.wait_ge(s_x1, k + 1)
                dve.nop(nofuse=True)
                for t in range(CT):
                    last = dve.bn_stats(stats2[:, t, :], x1[:, CT * k + t, :])
                last.then_inc(s_ln2, 1)
                dve.wait_ge(s_ln2, LN2 * k + 1)
                dve.nop(nofuse=True)
                for t in range(CT):
                    last = dve.bn_aggr(mv2[:, t, :], stats2[:, t, :])
                last.then_inc(s_ln2, 1)
                dve.wait_ge(s_ln2, LN2 * k + 2)
                dve.tensor_scalar(std2[:, 0, :], mv2[:, :, 1], EPS, None, ALU.add).then_inc(s_ln2, 1)

            def ln2_apply(k):
                dve.wait_ge(s_std2, k + 1)
                dve.reciprocal(std2[:, 2, :], std2[:, 1, :]).then_inc(s_ln2, 1)
                dve.wait_ge(s_ln2, LN2 * (k + 1))
                dve.wait_ge(s_x2c, k + 1)
                dve.wait_ge(s_x2t, k + 1)
                for t in range(CT):
                    last = dve.tensor_scalar(x2_cur[:, t, :], x1[:, CT * k + t, :], mv2[:, t, 0:1],
                                             std2[:, 2, t:t + 1], ALU.subtract, ALU.mult)
                last.then_inc(s_x2, 1)

            def logits_out(k):
                dve.wait_ge(s_lg, k + 1)
                dve.tensor_tensor(logits[:, ds(CT * k, CT), :], fin_ps[:, 0:CT * NE].rearrange("p (t e) -> p t e", t=CT),
                                  gb_bc[:, :].unsqueeze(1).broadcast_to([P, CT, NE]), ALU.add).then_inc(s_lgd, 1)

            def slots(k, b, h, prep, fin):
                for s in range(S):
                    if prep and s < 2:
                        mask(k + 1, 2 * s)
                        mask(k + 1, 2 * s + 1)
                    if prep and s == 7:
                        ln1_stats(k + 1, b + h, 1 - h)
                    if prep and s == 10:
                        ln1_apply(k + 1, 1 - h)
                    if prep and s == 13:
                        lo_part(k + 1, 1 - h)
                    if fin and s == 4:
                        gnn_out(k - 1, 1 - h)
                        ln2_stats(k - 1)
                    if fin and s == 7:
                        ln2_apply(k - 1)
                    if fin and s == 13:
                        logits_out(k - 1)
                    if prep and s == 20:
                        agg_init(k + 1, 1 - h)
                    ahead = s + NRING - 1
                    if ahead < S:
                        make_onehot(k, h, ahead)
                    elif prep:
                        make_onehot(k + 1, 1 - h, ahead - S)
                    take_max(k, h, s)

            dve.sem_inc(s_lgd, 1)
            ln1_stats(0, 0, 0)
            for i in range(CT):
                mask(0, i)
            ln1_apply(0, 0)
            lo_part(0, 0)
            agg_init(0, 0)
            for s in range(NRING - 1):
                make_onehot(0, 0, s)
            chunks(dve, slots)
            gnn_out(NCHUNK - 1, 1)
            ln2_stats(NCHUNK - 1)
            ln2_apply(NCHUNK - 1)
            logits_out(NCHUNK - 1)

            chain = [0]

            def link(ins):
                chain[0] += 1
                ins.then_inc(s_rc, 1)
                dve.wait_ge(s_rc, chain[0])

            def over_e(v):
                return v.unsqueeze(2).broadcast_to([P, TILES, NE])

            def over_t(v):
                return v.unsqueeze(1).broadcast_to([P, TILES, NE])

            def first_best(src, best, index, onehot_e):
                link(dve.tensor_reduce(best, src, AX.X, ALU.max))
                link(dve.tensor_tensor(eqi, src, over_e(best), ALU.is_equal))
                link(dve.tensor_tensor(eqi, eqi, over_t(iota_m[:, :]), ALU.mult))
                link(dve.tensor_reduce(index, eqi, AX.X, ALU.min))
                link(dve.tensor_tensor(onehot_e, over_t(iota_m[:, :]), over_e(index), ALU.is_equal))

            dve.wait_ge(s_lgd, NCHUNK + 1)
            dve.wait_ge(s_const, N_CONST)
            dve.wait_ge(s_rev, NB * NCHUNK)
            first_best(logits[:, :, :], small[:, 0, :], small[:, 4, :], oh1)
            link(dve.scalar_tensor_tensor(out=lmask, in0=oh1, scalar=-BIG, in1=logits[:, :, :],
                                          op0=ALU.mult, op1=ALU.add))
            first_best(lmask, small[:, 1, :], small[:, 5, :], oh2)
            dve.tensor_tensor(small[:, 2, :], small[:, 1, :], small[:, 0, :], ALU.subtract).then_inc(s_diff, 1)
            dve.wait_ge(s_parts, NCHUNK)
            dve.tensor_tensor(sel16.rearrange("p (t e) -> p t e", e=NE), oh1, oh2, ALU.add).then_inc(s_sel, 1)
            dve.wait_ge(s_exp, 1)
            link(dve.tensor_scalar(small[:, 6, :], small[:, 3, :], 1.0, None, ALU.add))
            link(dve.reciprocal(weight[:, 0, :], small[:, 6, :]))
            link(dve.tensor_tensor(weight[:, 1, :], small[:, 3, :], weight[:, 0, :], ALU.mult))
            dve.wait_ge(s_cntp, 1)
            for q in range(RN // CH):
                tq = CH // NE
                link(dve.tensor_copy(in_tile[:, q * tq:(q + 1) * tq, :], bank[q][:, :].rearrange("p (t e) -> p t e", e=NE)))
                link(dve.tensor_copy(tile_tot[:, q * tq:(q + 1) * tq, :], bank[2 + q][:, :].rearrange("p (t e) -> p t e", e=NE)))
            link(dve.memset(small[:, 7, :], 1.0))
            for e in range(NE):
                last = dve.tensor_tensor_scan(tile_inc[:, :, e], small[:, 7, :], tile_tot[:, :, e], 0.0, ALU.mult, ALU.add)
            link(last)
            link(dve.tensor_scalar(cnt[:, 0, :], tile_inc[:, TILES - 1, :], float(P - 1), None, ALU.add))
            link(dve.tensor_copy(cnt_i[:, 0, :], cnt[:, 0, :]))
            link(dve.tensor_scalar(cnt_i[:, 1, :], cnt_i[:, 0, :], 7, None, ALU.logical_shift_right))
            link(dve.tensor_copy(cnt[:, 1, :], cnt_i[:, 1, :]))
            link(dve.tensor_tensor_scan(cnt[:, 2, :], small[:, 7, 0:NE], cnt[:, 1, :], 0.0, ALU.mult, ALU.add))
            link(dve.tensor_tensor(cnt[:, 3, :], cnt[:, 2, :], cnt[:, 1, :], ALU.subtract))
            link(dve.tensor_scalar(cnt[:, 4, :], cnt[:, 3, :], float(P), None, ALU.mult))
            link(dve.tensor_tensor(pos_e, tile_inc, tile_tot, ALU.subtract))
            link(dve.tensor_tensor(pos_e, pos_e, in_tile, ALU.add))
            link(dve.tensor_tensor(pos_e, pos_e, over_t(cnt[:, 4, :]), ALU.add))
            for c, o in enumerate((oh1, oh2)):
                link(dve.tensor_tensor(o, o, pos_e, ALU.mult))
                link(dve.tensor_reduce(small[:, 8 + c, :], o, AX.X, ALU.add))
                link(dve.tensor_copy(pos_i[:, c, :], small[:, 8 + c, :]))
            dve.sem_inc(s_pos, 1)
            half = PAIR_TILES // 2
            for q in range(2):
                cv = cmp_j[:, 0:half * NE].rearrange("p (j e) -> p j e", e=NE)
                jv = iota_j[:, q * half:(q + 1) * half]
                link(dve.tensor_tensor(cv, cnt[:, 2, :].unsqueeze(1).broadcast_to([P, half, NE]),
                                       jv.unsqueeze(2).broadcast_to([P, half, NE]), ALU.is_le))
                link(dve.tensor_reduce(expert_f[:, q * half:(q + 1) * half], cv, AX.X, ALU.add))
            link(dve.tensor_scalar(expert_f[:, :], expert_f[:, :], float(NE - 1), None, ALU.min))
            link(dve.tensor_copy(expert_i[:, :], expert_f[:, :]))
            dve.sem_inc(s_pos, 1)

            def hidden(j, u):
                dve.wait_ge(s_silu, j + 1)
                wait(dve, s_ht, j - 1)
                dve.tensor_tensor(hid[:, u % 2, :], bank[2 + u % 2][:, HID:2 * HID], silu[:, u % 2, :], ALU.mult)\
                    .then_inc(s_hid, 1)

            def evac_hidden(j, u):
                dve.wait_ge(s_ht, j + 1)
                wait(dve, s_y, j - 1)
                dve.tensor_copy(hid_t[:, u % 2, :], bank[4][:, 0:HID]).then_inc(s_htev, 1)

            def expert_tile(j, u, last=False):
                evac_hidden(j, u)
                if not last:
                    hidden(j + 1, (u + 1) % 4)

            hidden(0, 0)
            for u in range(4):
                expert_tile(u, u)
            with dve.Fori(1, PAIR_TILES // 4 - 1) as i:
                for u in range(4):
                    expert_tile(4 * i + u, u)
            for u in range(4):
                expert_tile(PAIR_TILES - 4 + u, u, last=u == 3)

            for t in range(TILES):
                g = t % GB
                dve.wait_ge(s_g[g], 32 * (t // GB + 1))
                if t >= GB:
                    dve.wait_ge(s_out[g], 16 * (t // GB))
                dve.scalar_tensor_tensor(out=res_t[:, g, :], in0=yg[:, 2 * g, :], scalar=weight[:, 0, t:t + 1],
                                         in1=x1[:, t, :], op0=ALU.mult, op1=ALU.add).then_inc(s_c1, 1)
                dve.wait_ge(s_c1, t + 1)
                dve.scalar_tensor_tensor(out=res[:, g, :], in0=yg[:, 2 * g + 1, :], scalar=weight[:, 1, t:t + 1],
                                         in1=res_t[:, g, :], op0=ALU.mult, op1=ALU.add).then_inc(s_res, 1)

        @block.tensor
        def _(pe):
            def transpose_mask(k, q):
                pe.wait_ge(s_mask, CT * (k + 1))
                wait(pe, s_tev, NPIECE * k + q)
                for c in range(PIECE):
                    j = PIECE * q + c
                    for i in range(CT):
                        last = pe.transpose(tr_ps[:, c, i * P:(i + 1) * P], mask_nm[:, i, j * P:(j + 1) * P], ident16[:, :])
                last.then_inc(s_tr, 1)

            def rank_product(k, j):
                pe.wait_ge(s_tev, NPIECE * (k + 1))
                if j == 0:
                    wait(pe, s_init, k)
                else:
                    pe.wait_ge(s_rev, NB * k + j)
                for i in range(min(j + 1, NB)):
                    last = pe.matmul(rk_ps[:, :], (rank_mat if i == j else ones)[:, :], mask_t[:, i, :],
                                     start=(i == 0), stop=(i == min(j, NB - 1)))
                last.then_inc(s_rk, 1)

            def slot_product(k, h, s):
                if s == 0:
                    pe.wait_ge(s_parts, k + 1)
                pe.wait_ge(s_oh, S * k + s + 1)
                wait(pe, s_max, S * k + s - NRING + 1)
                for j in range(NB):
                    for part in range(2):
                        last = pe.matmul(bank[s % NRING][:, :], xparts[:, h, j, part, :],
                                         onehot[:, s % NRING, j * CH:(j + 1) * CH],
                                         start=(j == 0 and part == 0), stop=(j == NB - 1 and part == 1))
                last.then_inc(s_slot, 1)

            def transpose_xs(k, h):
                pe.wait_ge(s_lgd, k + 1)
                for i in range(CT):
                    last = pe.transpose(fin_ps[:, i * P:(i + 1) * P], xs[:, h, CT * h + i, :], ident32[:, :])
                last.then_inc(s_xt, 1)

            def gnn_product(k, h):
                pe.wait_ge(s_xtev, k + 1)
                pe.wait_ge(s_max, S * (k + 1))
                for i in range(CT):
                    pe.matmul(fin_ps[:, i * P:(i + 1) * P], xs_t[:, i * P:(i + 1) * P], w_gnn[:, 0, :], start=True, stop=False)
                    last = pe.matmul(fin_ps[:, i * P:(i + 1) * P], agg[:, h, i * P:(i + 1) * P], w_gnn[:, 1, :],
                                     start=False, stop=True)
                last.then_inc(s_fin, 1)

            def transpose_x2(k):
                pe.wait_ge(s_x2, k + 1)
                for i in range(CT):
                    last = pe.transpose(fin_ps[:, i * P:(i + 1) * P], x2_cur[:, i, :], ident32[:, :])
                last.then_inc(s_x2t, 1)

            def logit_product(k):
                pe.wait_ge(s_x2tev, k + 1)
                for i in range(CT):
                    last = pe.matmul(fin_ps[:, i * NE:(i + 1) * NE], x2_t[:, i * P:(i + 1) * P], gw[:, :], start=True, stop=True)
                last.then_inc(s_lg, 1)

            def slots(k, b, h, prep, fin):
                for s in range(S):
                    if prep and s % 2 == 1 and 3 <= s < 3 + 2 * NPIECE:
                        transpose_mask(k + 1, (s - 3) // 2)
                    if prep and 11 <= s <= 11 + NB:
                        rank_product(k + 1, s - 11)
                    if fin and s == 1:
                        transpose_xs(k - 1, 1 - h)
                    if fin and s == 3:
                        gnn_product(k - 1, 1 - h)
                    if fin and s == 9:
                        transpose_x2(k - 1)
                    if fin and s == 11:
                        logit_product(k - 1)
                    slot_product(k, h, s)

            pe.sem_inc(s_x2t, 1)
            pe.wait_ge(s_const, N_CONST)
            pe.wait_ge(s_w, 64)
            for q in range(NPIECE):
                transpose_mask(0, q)
            for j in range(NB + 1):
                rank_product(0, j)
            chunks(pe, slots)
            transpose_xs(NCHUNK - 1, 1)
            gnn_product(NCHUNK - 1, 1)
            transpose_x2(NCHUNK - 1)
            logit_product(NCHUNK - 1)

            pe.wait_ge(s_sel, 1)
            for q in range(RN // CH):
                pe.matmul(bank[q][:, :], tri[:, :], sel16[:, q * CH:(q + 1) * CH], start=True, stop=True)
                last = pe.matmul(bank[2 + q][:, :], ones[:, :], sel16[:, q * CH:(q + 1) * CH], start=True, stop=True)
            last.then_inc(s_cntp, 1)

            def transpose_rows(j, u, turn):
                pe.wait_ge(s_xd[u], 16 * turn)
                wait(pe, s_xdtev, j - 1)
                pe.transpose(bank[u % 2][:, 0:P], xd[:, u, :], ident32[:, :]).then_inc(s_xdt, 1)

            def hidden_product(j, u):
                e = pe.value_load(expert_i[0:1, ds(j, 1)], min_val=0, max_val=NE - 1)
                pe.wait_ge(s_xdtev, j + 1)
                wait(pe, s_hid, j - 1)
                pe.matmul(bank[2 + u % 2][:, :], xd_t[:, u % 2, :], w12[:, ds(e, 1), :].rearrange("p a h -> p (a h)"),
                          start=True, stop=True).then_inc(s_h, 1)

            def transpose_hidden(j, u):
                pe.wait_ge(s_hid, j + 1)
                wait(pe, s_htev, j)
                for c in range(2):
                    last = pe.transpose(bank[4][:, c * P:(c + 1) * P], hid[:, u % 2, c * P:(c + 1) * P], ident32[:, :])
                last.then_inc(s_ht, 1)

            def output_product(j, u):
                e = pe.value_load(expert_i[0:1, ds(j, 1)], min_val=0, max_val=NE - 1)
                pe.wait_ge(s_htev, j + 1)
                wait(pe, s_yev, j - 1)
                for c in range(2):
                    last = pe.matmul((rk_ps, fin_ps)[u % 2][:, 0:P], hid_t[:, u % 2, c * P:(c + 1) * P],
                                     w3_sb[:, ds(e, 1), c, :].rearrange("p a o -> p (a o)"), start=(c == 0), stop=(c == 1))
                last.then_inc(s_y, 1)

            def expert_tile(j, u, turn, left=99):
                if left > 1:
                    hidden_product(j + 1, (u + 1) % 4)
                transpose_hidden(j, u)
                if left > 2:
                    transpose_rows(j + 2, (u + 2) % 4, turn + (u + 2) // 4 + 1)
                output_product(j, u)

            pe.wait_ge(s_pos, 2)
            pe.wait_ge(s_wexp, 64)
            transpose_rows(0, 0, 1)
            transpose_rows(1, 1, 1)
            hidden_product(0, 0)
            for u in range(4):
                expert_tile(u, u, 0)
            with pe.Fori(1, PAIR_TILES // 4 - 1) as i:
                for u in range(4):
                    expert_tile(4 * i + u, u, i)
            for u in range(4):
                expert_tile(PAIR_TILES - 4 + u, u, PAIR_TILES // 4 - 1, left=4 - u)


def kernel(**inputs):
    import numpy as _np
    import concourse.bacc as _bacc
    from concourse import mybir as _mybir
    from concourse.bass_utils import run_bass_kernel_spmd as _run

    names = ["x", "adj", "L0_gnn_W", "L0_gnn_b", "L0_ffn_gate_w", "L0_ffn_gate_b", "L0_ffn_w1", "L0_ffn_w2", "L0_ffn_w3"]
    nc = _bacc.Bacc("TRN2", target_bir_lowering=False, num_devices=1)
    arrays, args = {}, []
    for name in names:
        a = _np.ascontiguousarray(inputs[name])
        arrays[f"in_{name}"] = a
        args.append(nc.dram_tensor(f"in_{name}", a.shape, _mybir.dt.from_np(a.dtype), kind="ExternalInput").ap())
    shape = inputs["x"].shape
    args.append(nc.dram_tensor("out_0", shape, _mybir.dt.float32, kind="ExternalOutput").ap())
    build(nc, *args)
    r = _run(nc, [arrays], core_ids=[0])
    return r.results[0]["out_0"]
```

```python
import concourse.bass as bass
from concourse import mybir
from contextlib import ExitStack
import numpy as np


def build(nc, x, adj, W, bias, gate_w, gate_b, w1, w2, w3, out):
    f32, f16, i32, u32 = mybir.dt.float32, mybir.dt.float16, mybir.dt.int32, mybir.dt.uint32
    ALU = mybir.AluOpType
    ACT = mybir.ActivationFunctionType
    AX = mybir.AxisListType
    ds = bass.ds

    P = 128
    B, N, C = x.shape
    NE, _, HID = w1.shape
    NB = N // P
    CH = 512
    CT = CH // P
    HALVES = N // CH
    NCHUNK = B * HALVES
    TILES = B * NB
    NEIGH = 25
    SG = 11
    S = NEIGH - SG
    SHIFT = 64
    PIECE = 2
    NPIECE = NB // PIECE
    NRING = 4
    EPS = 1e-5
    SCALE = 4096.0
    assert SCALE * np.sqrt(C - 1) < 65504 and NEIGH < SHIFT and HALVES == 2 and 8 < SG <= 16
    assert HALVES * S % NRING == 0 and S == 14
    BIG = 3.0e38
    PAIR_TILES = TILES * 2 + NE
    UN = 8
    TURNS = PAIR_TILES // UN
    assert PAIR_TILES % UN == 0
    TOKENS = TILES * P
    REGION = TOKENS + P
    PW = C + 1
    PAIRS = 2 * TOKENS
    FILL = NE * P

    x_rows = x.rearrange("b n c -> (b n) c")
    adj_rows = adj.rearrange("b n m -> (b n) m")
    out_rows = out.rearrange("b n c -> (b n) c")
    FEAT = N + 1
    feat = nc.dram_tensor("feat", (B * FEAT, C), f32).ap()
    dispatched = nc.dram_tensor("dispatched", (NE * REGION + FILL, PW), f32).ap()
    pair_rows = nc.dram_tensor("pair_rows", (PAIRS + 2 * FILL, C), f32).ap()

    ctx = ExitStack()
    with ctx:
        def sb(name, shape, dt):
            return ctx.enter_context(nc.sbuf_tensor(name, shape, dt))

        def sem(name):
            return ctx.enter_context(nc.semaphore(name))

        x1 = sb("x1", [P, TILES, C], f32)
        adj_in = sb("adj_in", [P, CT, N], i32)
        score = sb("score", [P, CT, N], f16)
        score2 = sb("score2", [P, CT, N], f16)
        falling = sb("falling", [P, N], f16)
        first = sb("first", [P, CT, 16], f16)
        nb_row = sb("nb_row", [P, 2, CT, 16], i32)
        feat_end = sb("feat_end", [P, 1], f32)
        near = sb("near", [P, CT, SG, C], f32)
        near_max = sb("near_max", [P, CT, C], f32)
        mask_t = sb("mask_t", [P, NB, CH], f16)
        rank_t = sb("rank_t", [P, 2, NB, CH], f16)
        onehot = sb("onehot", [P, NRING, NB * CH], f16)
        xparts = sb("xparts", [P, 2, NB, 2, C], f16)
        xin = sb("xin", [P, 2, NB, C], f32)
        xs = sb("xs", [P, 2, NB, C], f32)
        agg = sb("agg", [P, 2, CH], f32)
        xs_t = sb("xs_t", [P, CH], f32)
        gnn_tmp = sb("gnn_tmp", [P, CT, C], f32)
        pay = sb("pay", [P, 2, 2, CT, PW], f32)
        x2_t = xs_t
        fill = sb("fill", [P, NE, PW], f32)
        stats1 = sb("stats1", [P, NB, 6], f32)
        mv1 = sb("mv1", [P, NB, 2], f32)
        std1 = sb("std1", [P, 3, NB], f32)
        stats2 = sb("stats2", [P, CT, 6], f32)
        mv2 = sb("mv2", [P, CT, 2], f32)
        std2 = sb("std2", [P, 3, CT], f32)
        w_gnn = sb("w_gnn", [P, 2, C], f32)
        bias_bc = sb("bias_bc", [P, C], f32)
        gw = sb("gw", [P, NE], f32)
        gb_bc = sb("gb_bc", [P, NE], f32)
        ident16 = sb("ident16", [P, P], f16)
        ident32 = sb("ident32", [P, P], f32)
        rank_mat = sb("rank_mat", [P, P], f16)
        tri = sb("tri", [P, P], f16)
        ones = sb("ones", [P, P], f16)
        iota_m = sb("iota_m", [P, NE], f32)
        iota_p = sb("iota_p", [P, 1], f32)
        region = sb("region", [P, NE], f32)
        logits = sb("logits", [P, NB, NE], f32)
        lmask = sb("lmask", [P, NB, NE], f32)
        eqi = sb("eqi", [P, NB, NE], f32)
        oh = sb("oh", [P, 2, NB, NE], f32)
        pos_e = sb("pos_e", [P, NB, NE], f32)
        best = sb("best", [P, 4, NB], f32)
        pos_f = sb("pos_f", [P, 2, NB], f32)
        pos_i = sb("pos_i", [P, 2, NB], i32)
        sel16 = sb("sel16", [P, NB, NE], f16)
        taken = sb("taken", [P, NE], f32)
        gap = sb("gap", [P, TILES], f32)
        gap_exp = sb("gap_exp", [P, TILES], f32)
        weight = sb("weight", [P, 3, TILES], f32)
        w12 = onehot[:, :, :].rearrange("p r f -> p (r f)").bitcast(f32).rearrange("p (e h) -> p e h", e=NE)
        w3_sb = adj_in[:, :, :].rearrange("p t n -> p (t n)").bitcast(f32).rearrange("p (e k o) -> p e k o", e=NE, k=2)
        cnt = sb("cnt", [P, 7, NE], f32)
        cnt_i = sb("cnt_i", [P, 3, NE], i32)
        cnt_fill = cnt_i[:, 2, :]
        xi = xs[:, :, :, :].rearrange("p a b c -> p (a b c)")
        halfj = PAIR_TILES // 2
        ends = xi[:, 0:halfj * NE].rearrange("p (j e) -> p j e", e=NE)
        tile_f = sb("tile_f", [P, 4, PAIR_TILES], f32)
        tile_i = sb("tile_i", [P, 2, PAIR_TILES], i32)
        mt = mask_t[:, :, :].rearrange("p a b -> p (a b)").bitcast(f32)
        silu, hid, hid_t = (mt[:, i * 2 * HID:(i + 1) * 2 * HID].rearrange("p (r h) -> p r h", r=2) for i in range(3))
        xd_t = mt[:, 6 * HID:6 * HID + 2 * P].rearrange("p (r c) -> p r c", r=2)
        sc = score[:, :, :].rearrange("p a b -> p (a b)").bitcast(f32)
        xd = sc[:, 0:UN * PW].rearrange("p (r c) -> p r c", r=UN)
        sc2 = score2[:, :, :].rearrange("p a b -> p (a b)").bitcast(f32)
        yd = sc2[:, 0:UN * C].rearrange("p (r c) -> p r c", r=UN)
        pair_i = sb("pair_i", [P, UN], i32)
        QT = 4
        GB = 3
        nr = near[:, :, :, :].rearrange("p a b c -> p (a b c)")
        pairs_in = nr[:, 0:GB * QT * 2 * C].rearrange("p (g t c) -> p g t c", g=GB, t=QT)
        rtm = rank_t[:, :, :, :].rearrange("p a b c -> p (a b c)").bitcast(f32)
        part = rtm[:, 0:GB * QT * C].rearrange("p (g t c) -> p g t c", g=GB, t=QT)
        res = rtm[:, GB * QT * C:2 * GB * QT * C].rearrange("p (g t c) -> p g t c", g=GB, t=QT)

        bank = [ctx.enter_context(nc.psum_tensor(f"slot{i}", [P, CH], f32)) for i in range(NRING)]
        tr_ps = ctx.enter_context(nc.psum_tensor("tr_ps", [P, PIECE, CH], f16))
        rk_ps = [ctx.enter_context(nc.psum_tensor(f"rk_ps{i}", [P, CH], f32)) for i in range(2)]
        fin_ps = ctx.enter_context(nc.psum_tensor("fin_ps", [P, CH], f32))
        hid_t_ps, y_ps = rk_ps[0], (rk_ps[1], fin_ps)

        s_w = sem("weights_loaded")
        s_const = sem("constants_ready")
        s_absent = sem("absent_rows_stored")
        s_fill = sem("fill_stored")
        s_adj = [sem(f"adj_loaded{i}") for i in range(CT)]
        s_x = [sem(f"x_loaded{i}") for i in range(2)]
        s_feat = sem("features_stored")
        s_score = sem("score_done")
        s_top = sem("top_chain")
        s_row = sem("neighbour_rows_ready")
        s_near = [sem(f"gathered{i}") for i in range(CT)]
        s_red = sem("near_max_done")
        s_tr = sem("score_transposed")
        s_tev = sem("mask_t_done")
        s_rk = sem("rank_product_done")
        s_rev = sem("rank_t_done")
        s_init = sem("agg_started")
        s_oh = sem("onehot_done")
        s_slot = sem("slot_product_done")
        s_max = sem("max_done")
        s_ln1 = sem("ln1_chain")
        s_std1 = sem("std1_done")
        s_hi = sem("hi_part_done")
        s_parts = sem("x_parts_done")
        s_xt = sem("xs_transposed")
        s_xtev = sem("xs_t_done")
        s_nt = sem("near_max_transposed")
        s_agg = sem("agg_complete")
        s_fin = sem("gnn_product_done")
        s_tmp = sem("gnn_tmp_done")
        s_x1 = sem("x1_done")
        s_ln2 = sem("ln2_chain")
        s_std2 = sem("std2_done")
        s_pay = sem("pay_first_done")
        s_pay2 = sem("pay_second_done")
        s_x2t = sem("x2_transposed")
        s_x2tev = sem("x2_t_done")
        s_lg = sem("logit_product_done")
        s_lgd = sem("logits_done")
        s_rc = sem("routing_chain")
        s_sel = sem("sel_ready")
        s_route = sem("route_product_done")
        s_routed = sem("route_product_read")
        s_pos = sem("positions_ready")
        s_scat = sem("scattered")
        s_sent = sem("batch_scattered")
        s_cc = sem("counting_chain")
        s_exp = sem("exp_done")
        s_wexp = sem("expert_weights_loaded")
        s_filled = sem("tiles_filled")
        s_map = sem("tile_map_ready")
        s_fe = sem("feat_end_ready")
        s_filled_at = sem("filling_rows_known")
        s_gaps = sem("gap_written")
        s_share = sem("shares_chain")
        s_xd = [sem(f"rows_loaded{i}") for i in range(UN)]
        s_xdt = sem("rows_transposed")
        s_xdtev = sem("rows_t_done")
        s_pid = sem("pair_number_done")
        s_h = sem("hidden_product_done")
        s_silu = sem("silu_done")
        s_hid = sem("hidden_done")
        s_ht = sem("hidden_transposed")
        s_htev = sem("hidden_t_done")
        s_y = sem("expert_product_done")
        s_yev = sem("expert_rows_ready")
        s_yst = [sem(f"expert_rows_scattered{i}") for i in range(UN)]
        s_g = [sem(f"pairs_loaded{i}") for i in range(GB)]
        s_c1 = sem("combine_first")
        s_res = sem("result_ready")
        s_out = [sem(f"out_stored{i}") for i in range(GB)]

        def wait(eng, s, value):
            if not (isinstance(value, int) and value <= 0):
                eng.wait_ge(s, value)

        def chunks(eng, slots):
            slots(0, 0, 0, True, False)
            with eng.Fori(0, B - 1) as b:
                slots(2 * b + 1, b, 1, True, True)
                slots(2 * b + 2, b + 1, 0, True, True)
            slots(NCHUNK - 1, B - 1, 1, False, True)

        def expert_turns(eng, tiles):
            tiles(0, 0, 2 * UN)
            tiles(UN, 1, 2 * UN)
            with eng.Fori(2, TURNS - 1) as i:
                tiles(UN * i, i, 2 * UN)
            tiles(PAIR_TILES - UN, TURNS - 1, UN)

        N_CONST = 19
        LN1_VAR, LN1 = 3, 5
        LN2_VAR, LN2 = 3, 4
        TOP = 3
        RC_A, RC_B = 11, 6
        RC = RC_A + RC_B

        block = ctx.enter_context(nc.Block())

        @block.sync
        def _(sp):
            def load_x(k, b, h):
                wait(sp, s_x1, k - 1)
                sp.dma_start(xin[:, h, :, :], x_rows[ds(b * N, N), :].rearrange("(t p) c -> p t c", p=P))\
                    .then_inc(s_x[h], 16)

            def load_adj(k, i):
                wait(sp, s_score, CT * (k - 1) + i + 1)
                sp.dma_start(adj_in[:, i, :], adj_rows[ds(k * CH + i * P, P), :]).then_inc(s_adj[i], 16)

            def store_features(k, b):
                sp.wait_ge(s_ln1, LN1 * (k + 1))
                sp.dma_start(feat[ds(b * FEAT, N), :].rearrange("(t p) c -> p t c", p=P), xs[:, 0, :, :])\
                    .then_inc(s_feat, 16)

            load_x(0, 0, 0)
            for i in range(CT):
                load_adj(0, i)
            sp.dma_start(w_gnn[:, :, :], W.rearrange("(k p) o -> p k o", p=P)).then_inc(s_w, 16)
            sp.dma_start(bias_bc[:, :], bias.rearrange("(a o) -> a o", a=1).broadcast_to([P, C])).then_inc(s_w, 16)
            sp.dma_start(gw[:, :], gate_w).then_inc(s_w, 16)
            sp.dma_start(gb_bc[:, :], gate_b.rearrange("(a o) -> a o", a=1).broadcast_to([P, NE])).then_inc(s_w, 16)
            sp.wait_ge(s_const, N_CONST)
            for i in range(B * N // FILL):
                sp.dma_start(feat[i * FILL:(i + 1) * FILL, :].rearrange("(e p) c -> p e c", p=P),
                             fill[:, :, 0:C]).then_inc(s_absent, 16)
            sp.dma_start(feat[B * N:B * FEAT, :], fill[0:B, 0, 0:C]).then_inc(s_absent, 16)
            sp.wait_ge(s_absent, 16 * (B * N // FILL + 1))
            store_features(0, 0)
            for i in range(CT):
                load_adj(1, i)
            load_x(1, 0, 1)
            sp.dma_start(dispatched[NE * REGION:NE * REGION + FILL, :].rearrange("(e p) c -> p e c", p=P),
                         fill[:, :, :]).then_inc(s_fill, 16)
            with sp.Fori(0, B - 1) as b:
                for i in range(CT):
                    load_adj(2 * b + 2, i)
                load_x(2 * b + 2, b + 1, 0)
                store_features(2 * b + 2, b + 1)
                for i in range(CT):
                    load_adj(2 * b + 3, i)
                load_x(2 * b + 3, b + 1, 1)

            sp.wait_ge(s_score, CT * NCHUNK)
            for k in range(2):
                sp.dma_start(w3_sb[:, :, k, :], w3[:, k * P:(k + 1) * P, :].rearrange("e h o -> h e o"))\
                    .then_inc(s_wexp, 16)
            sp.wait_ge(s_slot, S * NCHUNK)
            sp.dma_start(w12[:, :, 0:HID], w1.rearrange("e d h -> d e h")).then_inc(s_wexp, 16)
            sp.dma_start(w12[:, :, HID:2 * HID], w2.rearrange("e d h -> d e h")).then_inc(s_wexp, 16)

            def load_rows(j, u):
                row = sp.value_load(tile_i[0:1, 1, ds(j, 1)], min_val=0, max_val=NE * REGION + FILL - P)
                wait(sp, s_xdt, j - UN + 1)
                if not isinstance(j, int) or j >= UN:
                    sp.wait_ge(s_pid, j - UN + 1)
                sp.dma_start(xd[:, u, :], dispatched[ds(row, P), :]).then_inc(s_xd[u], 16)

            sp.wait_ge(s_map, 1)
            sp.wait_ge(s_filled, NE * 16)
            sp.wait_ge(s_scat, 2 * TILES * 16)
            sp.wait_ge(s_fill, 16)
            for u in range(UN):
                load_rows(u, u)
            with sp.Fori(1, TURNS) as i:
                for u in range(UN):
                    load_rows(UN * i + u, u)

            for u in range(UN):
                sp.wait_ge(s_yst[u], 16 * TURNS)
            quads = TILES // QT

            def load_pairs(q):
                if q >= GB:
                    sp.wait_ge(s_res, QT * (q - GB + 1))
                sp.dma_start(pairs_in[:, q % GB, :, :],
                             pair_rows[2 * q * QT * P:2 * (q + 1) * QT * P, :].rearrange("(t p c) d -> p t (c d)", p=P, c=2))\
                    .then_inc(s_g[q % GB], 16)

            for q in range(GB):
                load_pairs(q)
            for q in range(quads):
                sp.wait_ge(s_res, QT * (q + 1))
                sp.dma_start(out_rows[q * QT * P:(q + 1) * QT * P, :].rearrange("(t p) c -> p t c", p=P),
                             res[:, q % GB, :, :]).then_inc(s_out[q % GB], 16)
                if q + GB < quads:
                    load_pairs(q + GB)
            for g in range(GB):
                sp.wait_ge(s_out[g], 16 * len(range(g, quads, GB)))

        @block.gpsimd
        def _(pool):
            pool.sem_inc(s_sent, 1)
            n = [0]

            def done(ins):
                n[0] += 1
                ins.then_inc(s_const, 1)

            def iota(ap, pattern, base, channel_multiplier):
                done(pool.iota(ap, pattern=pattern, base=base, channel_multiplier=channel_multiplier,
                               allow_small_or_imprecise_dtypes=True))

            iota(falling[:, :], [[-1, N]], N, 0)
            done(pool.memset(ident16[:, :], 0.0))
            done(pool.memset(ident32[:, :], 0.0))
            done(pool.memset(rank_mat[:, :], 1.0))
            done(pool.memset(tri[:, :], 1.0))
            done(pool.memset(ones[:, :], 1.0))
            done(pool.memset(fill[:, :, 0:C], 0.0))
            pool.wait_ge(s_const, n[0])
            for m in (ident16, ident32):
                done(pool.affine_select(out=m[:, :], in_=m[:, :], compare_op=ALU.not_equal, fill=1.0, base=0,
                                        pattern=[[-1, P]], channel_multiplier=1))
            for m in (rank_mat, tri):
                done(pool.affine_select(out=m[:, :], in_=m[:, :], compare_op=ALU.is_gt, fill=0.0, base=0,
                                        pattern=[[1, P]], channel_multiplier=-1))
            pool.wait_ge(s_const, n[0])
            done(pool.affine_select(out=rank_mat[:, :], in_=rank_mat[:, :], compare_op=ALU.not_equal,
                                    fill=-float(SHIFT), base=0, pattern=[[-1, P]], channel_multiplier=1))
            iota(iota_m[:, :], [[1, NE]], -64, 0)
            iota(iota_p[:, :], [[1, 1]], 0, 1)
            iota(region[:, :], [[REGION, NE]], 0, 0)
            iota(tile_f[:, 0, :], [[1, PAIR_TILES]], 0, 0)
            for h in range(2):
                iota(pay[:, :, h, :, C], [[1, 2], [2 * P, CT]], 2 * CH * h - 2 * N, 2)
            iota(fill[:, :, C], [[P, NE]], PAIRS + FILL, 1)

            def gather(k, h, i):
                if i == 0:
                    pool.wait_ge(s_row, k + 1)
                wait(pool, s_red, CT * (k - 1) + i + 1)
                pool.nop(nofuse=True)
                for c in range(SG):
                    pool.indirect_dma_start(
                        out=near[:, i, c, :], out_offset=None, in_=feat[:, :],
                        in_offset=bass.IndirectOffsetOnAxis(ap=nb_row[:, h, i, c:c + 1].bitcast(u32), axis=0))\
                        .then_inc(s_near[i], 16)

            def scatter(b):
                pool.wait_ge(s_pos, b + 1)
                pool.wait_ge(s_pay2, 2 * (b + 1))
                pool.nop(nofuse=True)
                for t in range(NB):
                    for c in range(2):
                        pool.indirect_dma_start(
                            out=dispatched[:, :], out_offset=bass.IndirectOffsetOnAxis(ap=pos_i[:, c, t:t + 1].bitcast(u32), axis=0),
                            in_=pay[:, c, t // CT, t % CT, :], in_offset=None).then_inc(s_scat, 16)
                pool.wait_ge(s_scat, 16 * 2 * NB * (b + 1))
                pool.sem_inc(s_sent, 1)

            def slots(k, b, h, prep, fin):
                if h == 0:
                    pool.wait_ge(s_feat, 16 * (b + 1))
                    pool.nop(nofuse=True)
                for i in range(CT):
                    gather(k, h, i)
                if h == 0 and fin:
                    scatter(b - 1)

            pool.wait_ge(s_fill, 16)
            done(pool.tensor_scalar(fill[:, :, C], fill[:, :, C], 1.0, -float(FILL), ALU.mult, ALU.add))
            assert n[0] == N_CONST + 1
            pool.wait_ge(s_absent, 16 * (B * N // FILL + 1))
            chunks(pool, slots)
            scatter(B - 1)

            pool.wait_ge(s_filled_at, 1)
            pool.wait_ge(s_const, N_CONST + 1)
            for e in range(NE):
                pool.indirect_dma_start(
                    out=dispatched[:, :], out_offset=bass.IndirectOffsetOnAxis(ap=cnt_fill[:, e:e + 1].bitcast(u32), axis=0),
                    in_=fill[:, e, :], in_offset=None).then_inc(s_filled, 16)

            def tiles(j0, turn, left):
                for u in range(UN):
                    pool.wait_ge(s_xd[u], 16 * (turn + 1))
                    wait(pool, s_yst[u], 16 * turn)
                    pool.nop(nofuse=True)
                    pool.tensor_copy(pair_i[:, u:u + 1], xd[:, u, C:C + 1]).then_inc(s_pid, 1)
                    pool.wait_ge(s_pid, j0 + u + 1)
                    pool.wait_ge(s_yev, j0 + u + 1)
                    pool.nop(nofuse=True)
                    pool.indirect_dma_start(
                        out=pair_rows[:, :], out_offset=bass.IndirectOffsetOnAxis(ap=pair_i[:, u:u + 1].bitcast(u32), axis=0),
                        in_=yd[:, u, :], in_offset=None).then_inc(s_yst[u], 16)

            expert_turns(pool, tiles)

        @block.scalar
        def _(act):
            def evac_mask(k, q):
                act.wait_ge(s_tr, NPIECE * k + q + 1)
                if q == 0:
                    wait(act, s_rk, (NB + 1) * k)
                act.activation(mask_t[:, PIECE * q:PIECE * (q + 1), :], tr_ps[:, :, :], ACT.Sign).then_inc(s_tev, 1)

            def evac_rank(k, h, j):
                act.wait_ge(s_rk, (NB + 1) * k + j + 1)
                if j == 0:
                    wait(act, s_oh, S * (k - 1))
                act.activation(rank_t[:, h, j, :], rk_ps[j % 2][:, :], ACT.Copy).then_inc(s_rev, 1)

            def root1(k):
                act.wait_ge(s_ln1, LN1 * k + LN1_VAR)
                act.activation(std1[:, 1, :], std1[:, 0, :], ACT.Sqrt).then_inc(s_std1, 1)

            def hi_part(k, h):
                act.wait_ge(s_ln1, LN1 * (k + 1))
                wait(act, s_slot, S * (k - 1))
                act.activation(xparts[:, h, :, 0, :], xs[:, h, :, :], ACT.Copy).then_inc(s_hi, 1)

            def evac_xs(k):
                act.wait_ge(s_xt, k + 1)
                act.activation(xs_t[:, :], fin_ps[:, :], ACT.Copy).then_inc(s_xtev, 1)

            def root2(k):
                act.wait_ge(s_ln2, LN2 * k + LN2_VAR)
                act.activation(std2[:, 1, :], std2[:, 0, :], ACT.Sqrt).then_inc(s_std2, 1)

            def second_pay(k, h):
                act.wait_ge(s_pay, k + 1)
                act.activation(pay[:, 1, h, :, 0:C], pay[:, 0, h, :, 0:C], ACT.Copy).then_inc(s_pay2, 1)

            def evac_x2(k):
                act.wait_ge(s_x2t, k + 1)
                act.activation(x2_t[:, :], fin_ps[:, :], ACT.Copy).then_inc(s_x2tev, 1)

            def slots(k, b, h, prep, fin):
                for s in range(S):
                    if fin and s == 1:
                        evac_xs(k - 1)
                    if prep and 2 <= s < 2 + NPIECE:
                        evac_mask(k + 1, s - 2)
                    if fin and s == 5:
                        root2(k - 1)
                    if prep and 6 <= s < 6 + NB // 2:
                        evac_rank(k + 1, 1 - h, 2 * (s - 6))
                        evac_rank(k + 1, 1 - h, 2 * (s - 6) + 1)
                    if fin and s == 7:
                        second_pay(k - 1, 1 - h)
                        evac_x2(k - 1)
                    if prep and s == 7:
                        root1(k + 1)
                    if prep and s == 9:
                        hi_part(k + 1, 1 - h)

            root1(0)
            hi_part(0, 0)
            for q in range(NPIECE):
                evac_mask(0, q)
            for j in range(NB):
                evac_rank(0, 0, j)
            chunks(act, slots)
            evac_xs(NCHUNK - 1)
            root2(NCHUNK - 1)
            second_pay(NCHUNK - 1, 1)
            evac_x2(NCHUNK - 1)

            act.wait_ge(s_gaps, B)
            act.activation(gap_exp[:, :], gap[:, :], ACT.Exp).then_inc(s_exp, 1)

            def evac_rows(j, u):
                act.wait_ge(s_xdt, j + 1)
                act.activation(xd_t[:, u % 2, :], bank[u % 2][:, 0:P], ACT.Copy).then_inc(s_xdtev, 1)

            def do_silu(j, u):
                act.wait_ge(s_h, j + 1)
                wait(act, s_hid, j - 1)
                act.activation(silu[:, u % 2, :], bank[2 + u % 2][:, 0:HID], ACT.Silu).then_inc(s_silu, 1)

            def evac_y(j, u, turn):
                act.wait_ge(s_y, j + 1)
                wait(act, s_yst[u], 16 * turn)
                act.activation(yd[:, u, :], y_ps[u % 2][:, 0:P], ACT.Copy).then_inc(s_yev, 1)

            def tiles(j0, turn, left):
                for u in range(UN):
                    j = j0 + u
                    if u + 1 < left:
                        do_silu(j + 1, u + 1)
                    if u or not isinstance(j0, int) or j0:
                        evac_y(j - 1, (u - 1) % UN, turn if u else turn - 1)
                    if u + 3 < left:
                        evac_rows(j + 3, u + 3)

            for u in range(3):
                evac_rows(u, u)
            do_silu(0, 0)
            expert_turns(act, tiles)
            evac_y(PAIR_TILES - 1, UN - 1, TURNS - 1)

        @block.vector
        def _(dve):
            def make_score(k, i):
                dve.wait_ge(s_adj[i], 16 * (k + 1))
                if i == 0:
                    wait(dve, s_tr, NPIECE * k)
                dve.scalar_tensor_tensor(out=score[:, i, :], in0=adj_in[:, i, :], scalar=0.0, in1=falling[:, :],
                                         op0=ALU.not_equal, op1=ALU.mult).then_inc(s_score, 1)

            def top_first(k):
                dve.wait_ge(s_score, CT * (k + 1))
                dve.nop(nofuse=True)
                for i in range(CT):
                    last = dve.max(first[:, i, 0:8], score[:, i, :])
                last.then_inc(s_top, 1)

            def top_drop(k, tiles_):
                dve.wait_ge(s_top, TOP * k + 1)
                dve.nop(nofuse=True)
                for i in tiles_:
                    last = dve.match_replace(score2[:, i, :], first[:, i, 0:8], score[:, i, :], 0.0)
                if tiles_[-1] == CT - 1:
                    last.then_inc(s_top, 1)

            def top_second(k):
                dve.wait_ge(s_top, TOP * k + 2)
                dve.nop(nofuse=True)
                for i in range(CT):
                    last = dve.max(first[:, i, 8:16], score2[:, i, :])
                last.then_inc(s_top, 1)

            def neighbour_rows(k, h):
                dve.wait_ge(s_top, TOP * (k + 1))
                if h == 0:
                    dve.tensor_scalar(feat_end[:, :], feat_end[:, :], float(FEAT), None, ALU.add).then_inc(s_fe, 1)
                dve.wait_ge(s_fe, batch_of[0] + 2)
                dve.tensor_scalar(nb_row[:, h, :, :], first[:, :, :], -1.0, feat_end[:, 0:1], ALU.mult, ALU.add)\
                    .then_inc(s_row, 1)

            batch_of = [0]

            def near_reduce(k, i):
                dve.wait_ge(s_near[i], 16 * SG * (k + 1))
                if i == 0:
                    wait(dve, s_nt, k)
                dve.tensor_reduce(near_max[:, i, :], near[:, i, :, :].rearrange("p s c -> p c s"), AX.X, ALU.max)\
                    .then_inc(s_red, 1)

            def agg_merge(k, h):
                dve.wait_ge(s_nt, k + 1)
                dve.wait_ge(s_max, S * (k + 1))
                dve.tensor_tensor(agg[:, h, :], fin_ps[:, :], agg[:, h, :], ALU.max).then_inc(s_agg, 1)

            def ln1_stats(k, b, h):
                dve.wait_ge(s_x[h], 16 * (b + 1))
                dve.nop(nofuse=True)
                for t in range(NB):
                    last = dve.bn_stats(stats1[:, t, :], xin[:, h, t, :])
                last.then_inc(s_ln1, 1)
                dve.wait_ge(s_ln1, LN1 * k + 1)
                dve.nop(nofuse=True)
                for t in range(NB):
                    last = dve.bn_aggr(mv1[:, t, :], stats1[:, t, :])
                last.then_inc(s_ln1, 1)
                dve.wait_ge(s_ln1, LN1 * k + 2)
                dve.tensor_scalar(std1[:, 0, :], mv1[:, :, 1], EPS, 1.0 / (SCALE * SCALE), ALU.add, ALU.mult)\
                    .then_inc(s_ln1, 1)

            def ln1_apply(k, h):
                dve.wait_ge(s_std1, k + 1)
                dve.reciprocal(std1[:, 2, :], std1[:, 1, :]).then_inc(s_ln1, 1)
                dve.wait_ge(s_ln1, LN1 * k + LN1_VAR + 1)
                wait(dve, s_xt, k - 1)
                if h == 0 and not isinstance(k, int):
                    dve.wait_ge(s_feat, 16 * batch_of[0])
                for t in range(NB):
                    last = dve.tensor_scalar(xs[:, h, t, :], xin[:, h, t, :], mv1[:, t, 0:1], std1[:, 2, t:t + 1],
                                             ALU.subtract, ALU.mult)
                last.then_inc(s_ln1, 1)

            def lo_part(k, h):
                dve.wait_ge(s_hi, k + 1)
                dve.tensor_tensor(xparts[:, h, :, 1, :], xs[:, h, :, :], xparts[:, h, :, 0, :], ALU.subtract)\
                    .then_inc(s_parts, 1)

            def agg_init(k, h):
                dve.wait_ge(s_rk, (NB + 1) * (k + 1))
                wait(dve, s_fin, k - 1)
                dve.tensor_scalar(agg[:, h, :], rk_ps[0][:, :], NEIGH + 0.5, -BIG, ALU.is_gt, ALU.mult).then_inc(s_init, 1)

            def make_onehot(k, h, s):
                if s == 0:
                    dve.wait_ge(s_rev, NB * (k + 1))
                wait(dve, s_slot, S * k + s - NRING + 1)
                dve.tensor_scalar(onehot[:, (S * h + s) % NRING, :], rank_t[:, h, :, :].rearrange("p a b -> p (a b)"),
                                  float(SG + s - SHIFT), None, ALU.is_equal).then_inc(s_oh, 1)

            def take_max(k, h, s):
                if s == 0:
                    dve.wait_ge(s_init, k + 1)
                dve.wait_ge(s_slot, S * k + s + 1)
                wait(dve, s_max, S * k + s)
                dve.tensor_tensor(agg[:, h, :], bank[(S * h + s) % NRING][:, :], agg[:, h, :], ALU.max).then_inc(s_max, 1)

            def gnn_out(k, h):
                dve.wait_ge(s_fin, k + 1)
                dve.scalar_tensor_tensor(out=gnn_tmp[:, :, :], in0=fin_ps[:, :].rearrange("p (t c) -> p t c", t=CT),
                                         scalar=1.0 / SCALE, in1=bias_bc[:, :].unsqueeze(1).broadcast_to([P, CT, C]),
                                         op0=ALU.mult, op1=ALU.add).then_inc(s_tmp, 1)
                dve.wait_ge(s_tmp, k + 1)
                dve.scalar_tensor_tensor(out=x1[:, ds(CT * k, CT), :], in0=gnn_tmp[:, :, :], scalar=0.0,
                                         in1=xin[:, h, CT * h:CT * h + CT, :], op0=ALU.max, op1=ALU.add)\
                    .then_inc(s_x1, 1)

            def ln2_stats(k):
                dve.wait_ge(s_x1, k + 1)
                dve.nop(nofuse=True)
                for t in range(CT):
                    last = dve.bn_stats(stats2[:, t, :], x1[:, CT * k + t, :])
                last.then_inc(s_ln2, 1)
                dve.wait_ge(s_ln2, LN2 * k + 1)
                dve.nop(nofuse=True)
                for t in range(CT):
                    last = dve.bn_aggr(mv2[:, t, :], stats2[:, t, :])
                last.then_inc(s_ln2, 1)
                dve.wait_ge(s_ln2, LN2 * k + 2)
                dve.tensor_scalar(std2[:, 0, :], mv2[:, :, 1], EPS, None, ALU.add).then_inc(s_ln2, 1)

            def ln2_apply(k, b, h):
                dve.wait_ge(s_std2, k + 1)
                dve.reciprocal(std2[:, 2, :], std2[:, 1, :]).then_inc(s_ln2, 1)
                dve.wait_ge(s_sent, b + 1)
                dve.tensor_scalar(pay[:, :, h, :, C], pay[:, :, h, :, C], float(2 * N), None, ALU.add)
                dve.wait_ge(s_ln2, LN2 * (k + 1))
                for t in range(CT):
                    last = dve.tensor_scalar(pay[:, 0, h, t, 0:C], x1[:, CT * k + t, :], mv2[:, t, 0:1],
                                             std2[:, 2, t:t + 1], ALU.subtract, ALU.mult)
                last.then_inc(s_pay, 1)

            def logits_out(k, h):
                dve.wait_ge(s_lg, k + 1)
                dve.tensor_tensor(logits[:, CT * h:CT * h + CT, :], fin_ps[:, 0:CT * NE].rearrange("p (t e) -> p t e", t=CT),
                                  gb_bc[:, :].unsqueeze(1).broadcast_to([P, CT, NE]), ALU.add).then_inc(s_lgd, 1)

            def over_e(v, rows=NB):
                return v.unsqueeze(2).broadcast_to([P, rows, NE])

            def over_t(v, rows=NB):
                return v.unsqueeze(1).broadcast_to([P, rows, NE])

            def chain(semaphore, base, steps):
                n = [0]

                def link(ins=None):
                    if ins is None:
                        assert n[0] == steps, n
                        return
                    n[0] += 1
                    ins.then_inc(semaphore, 1)
                    dve.wait_ge(semaphore, base + n[0])
                return link

            def route_first(b):
                link = chain(s_rc, RC * b, RC_A)
                dve.wait_ge(s_lgd, 2 * b + 3)
                for c, src in enumerate((logits[:, :, :], lmask[:, :, :])):
                    link(dve.tensor_reduce(best[:, c, :], src, AX.X, ALU.max))
                    link(dve.tensor_tensor(eqi[:, :, :], src, over_e(best[:, c, :]), ALU.is_equal))
                    link(dve.tensor_tensor(eqi[:, :, :], eqi[:, :, :], over_t(iota_m[:, :]), ALU.mult))
                    link(dve.tensor_reduce(best[:, 2 + c, :], eqi[:, :, :], AX.X, ALU.min))
                    link(dve.tensor_tensor(oh[:, c, :, :], over_t(iota_m[:, :]), over_e(best[:, 2 + c, :]), ALU.is_equal))
                    if c == 0:
                        link(dve.scalar_tensor_tensor(out=lmask[:, :, :], in0=oh[:, 0, :, :], scalar=-BIG,
                                                      in1=logits[:, :, :], op0=ALU.mult, op1=ALU.add))
                link()
                dve.tensor_tensor(sel16[:, :, :], oh[:, 0, :, :], oh[:, 1, :, :], ALU.add).then_inc(s_sel, 1)
                dve.tensor_tensor(gap[:, ds(NB * b, NB)], best[:, 1, :], best[:, 0, :], ALU.subtract).then_inc(s_gaps, 1)

            def route_second(b):
                link = chain(s_rc, RC * b + RC_A, RC_B)
                dve.wait_ge(s_route, b + 1)
                link(dve.tensor_tensor(pos_e[:, :, :], fin_ps[:, 0:NB * NE].rearrange("p (t e) -> p t e", e=NE),
                                       over_t(taken[:, :]), ALU.add))
                link(dve.tensor_tensor(taken[:, :], fin_ps[:, NB * NE:NB * NE + NE], taken[:, :], ALU.add))
                dve.sem_inc(s_routed, 1)
                for c in range(2):
                    last = dve.tensor_tensor(oh[:, c, :, :], oh[:, c, :, :], pos_e[:, :, :], ALU.mult)
                link(last)
                dve.wait_ge(s_sent, b + 1)
                link(dve.tensor_reduce(pos_f[:, 0, :], oh[:, 0, :, :], AX.X, ALU.add))
                link(dve.tensor_reduce(pos_f[:, 1, :], oh[:, 1, :, :], AX.X, ALU.add))
                link(dve.tensor_copy(pos_i[:, :, :], pos_f[:, :, :]))
                link()
                dve.sem_inc(s_pos, 1)

            def slots(k, b, h, prep, fin):
                fb = b if h else b - 1
                batch_of[0] = b + h
                for s in range(S):
                    if fin and s == 0:
                        near_reduce(k - 1, CT - 1)
                    if prep and s == 0:
                        for i in range(CT):
                            make_score(k + 1, i)
                    if prep and s == 1:
                        top_first(k + 1)
                    if fin and s == 2:
                        agg_merge(k - 1, 1 - h)
                    if prep and s == 2:
                        top_drop(k + 1, (0, 1))
                    if prep and s == 3:
                        top_drop(k + 1, (2, 3))
                    if fin and s == 4:
                        gnn_out(k - 1, 1 - h)
                        ln2_stats(k - 1)
                    if s == 5:
                        near_reduce(k, 0)
                    if fin and s == 5:
                        ln2_apply(k - 1, fb, 1 - h)
                    if prep and s == 6:
                        ln1_stats(k + 1, b + h, 1 - h)
                        top_second(k + 1)
                    if prep and s == 7:
                        neighbour_rows(k + 1, 1 - h)
                    if prep and s == 8:
                        ln1_apply(k + 1, 1 - h)
                    if fin and s == 8:
                        logits_out(k - 1, 1 - h)
                        near_reduce(k, 1)
                    elif s == 8:
                        near_reduce(k, 1)
                    if fin and h == 0 and s == 9:
                        route_first(fb)
                    if prep and s == 10:
                        lo_part(k + 1, 1 - h)
                    if s == 11:
                        near_reduce(k, 2)
                    if prep and s == 11:
                        agg_init(k + 1, 1 - h)
                    if fin and h == 0 and s == 12:
                        route_second(fb)
                    ahead = s + NRING - 1
                    if ahead < S:
                        make_onehot(k, h, ahead)
                    elif prep:
                        make_onehot(k + 1, 1 - h, ahead - S)
                    take_max(k, h, s)

            dve.sem_inc(s_lgd, 1)
            dve.sem_inc(s_routed, 1)
            dve.memset(feat_end[:, :], float(N - FEAT)).then_inc(s_fe, 1)
            dve.wait_ge(s_const, N_CONST)
            dve.tensor_copy(taken[:, :], region[:, :]).then_inc(s_cc, 1)
            ln1_stats(0, 0, 0)
            for i in range(CT):
                make_score(0, i)
            ln1_apply(0, 0)
            top_first(0)
            top_drop(0, range(CT))
            lo_part(0, 0)
            top_second(0)
            dve.wait_ge(s_fe, 1)
            neighbour_rows(0, 0)
            agg_init(0, 0)
            for s in range(NRING - 1):
                make_onehot(0, 0, s)
            dve.wait_ge(s_cc, 1)
            chunks(dve, slots)
            near_reduce(NCHUNK - 1, CT - 1)
            agg_merge(NCHUNK - 1, 1)
            gnn_out(NCHUNK - 1, 1)
            ln2_stats(NCHUNK - 1)
            ln2_apply(NCHUNK - 1, B - 1, 1)
            logits_out(NCHUNK - 1, 1)
            route_first(B - 1)
            route_second(B - 1)

            link = chain(s_cc, 1, 12 + 2 * 4)
            link(dve.tensor_scalar(cnt[:, 5, :], taken[:, :], iota_p[:, 0:1], None, ALU.add))
            dve.tensor_copy(cnt_fill, cnt[:, 5, :]).then_inc(s_filled_at, 1)
            link(dve.tensor_tensor(cnt[:, 6, :], taken[:, :], region[:, :], ALU.subtract))
            link(dve.tensor_scalar(cnt[:, 0, :], cnt[:, 6, :], float(P - 1), None, ALU.add))
            link(dve.tensor_copy(cnt_i[:, 0, :], cnt[:, 0, :]))
            link(dve.tensor_scalar(cnt_i[:, 1, :], cnt_i[:, 0, :], P.bit_length() - 1, None, ALU.logical_shift_right))
            link(dve.tensor_copy(cnt[:, 1, :], cnt_i[:, 1, :]))
            link(dve.memset(cnt[:, 3, :], 1.0))
            link(dve.tensor_tensor_scan(cnt[:, 2, :], cnt[:, 3, :], cnt[:, 1, :], 0.0, ALU.mult, ALU.add))
            for q in range(2):
                jj = slice(q * halfj, (q + 1) * halfj)
                link(dve.tensor_tensor(ends, over_t(cnt[:, 2, :], halfj), over_e(tile_f[:, 0, jj], halfj), ALU.is_le))
                link(dve.tensor_reduce(tile_f[:, 1, jj], ends, AX.X, ALU.add))
                link(dve.tensor_tensor(ends, ends, over_t(cnt[:, 1, :], halfj), ALU.mult))
                link(dve.tensor_reduce(tile_f[:, 2, jj], ends, AX.X, ALU.add))
            link(dve.tensor_tensor(tile_f[:, 3, :], tile_f[:, 0, :], tile_f[:, 2, :], ALU.subtract))
            link(dve.tensor_scalar(tile_f[:, 3, :], tile_f[:, 3, :], float(P), None, ALU.mult))
            link(dve.scalar_tensor_tensor(out=tile_f[:, 3, :], in0=tile_f[:, 1, :], scalar=float(REGION),
                                          in1=tile_f[:, 3, :], op0=ALU.mult, op1=ALU.add))
            dve.tensor_copy(tile_i[:, 1, :], tile_f[:, 3, :])
            link(dve.tensor_scalar(tile_i[:, 0, :], tile_f[:, 1, :], float(NE - 1), None, ALU.min))
            link()
            dve.sem_inc(s_map, 1)
            dve.wait_ge(s_exp, 1)
            dve.tensor_scalar(weight[:, 2, :], gap_exp[:, :], 1.0, None, ALU.add).then_inc(s_share, 1)
            dve.wait_ge(s_share, 1)
            dve.reciprocal(weight[:, 0, :], weight[:, 2, :]).then_inc(s_share, 1)
            dve.wait_ge(s_share, 2)
            dve.tensor_tensor(weight[:, 1, :], gap_exp[:, :], weight[:, 0, :], ALU.mult).then_inc(s_share, 1)

            def hidden(j, u):
                dve.wait_ge(s_silu, j + 1)
                wait(dve, s_ht, j - 1)
                dve.tensor_tensor(hid[:, u % 2, :], bank[2 + u % 2][:, HID:2 * HID], silu[:, u % 2, :], ALU.mult)\
                    .then_inc(s_hid, 1)

            def evac_hidden(j, u):
                dve.wait_ge(s_ht, j + 1)
                wait(dve, s_y, j - 1)
                dve.tensor_copy(hid_t[:, u % 2, :], hid_t_ps[:, 0:HID]).then_inc(s_htev, 1)

            def tiles(j0, turn, left):
                for u in range(UN):
                    if u + 1 < left:
                        hidden(j0 + u + 1, u + 1)
                    evac_hidden(j0 + u, u)

            hidden(0, 0)
            expert_turns(dve, tiles)

            dve.wait_ge(s_share, 3)
            for t in range(TILES):
                q, i = t // QT, t % QT
                g = q % GB
                if i == 0:
                    dve.wait_ge(s_g[g], 16 * (q // GB + 1))
                    if q >= GB:
                        dve.wait_ge(s_out[g], 16 * (q // GB))
                dve.scalar_tensor_tensor(out=part[:, g, i, :], in0=pairs_in[:, g, i, 0:C], scalar=weight[:, 0, t:t + 1],
                                         in1=x1[:, t, :], op0=ALU.mult, op1=ALU.add).then_inc(s_c1, 1)
                dve.wait_ge(s_c1, t + 1)
                dve.scalar_tensor_tensor(out=res[:, g, i, :], in0=pairs_in[:, g, i, C:2 * C], scalar=weight[:, 1, t:t + 1],
                                         in1=part[:, g, i, :], op0=ALU.mult, op1=ALU.add).then_inc(s_res, 1)

        @block.tensor
        def _(pe):
            def transpose_score(k, q):
                pe.wait_ge(s_score, CT * (k + 1))
                wait(pe, s_tev, NPIECE * k + q)
                for c in range(PIECE):
                    j = PIECE * q + c
                    for i in range(CT):
                        last = pe.transpose(tr_ps[:, c, i * P:(i + 1) * P], score[:, i, j * P:(j + 1) * P], ident16[:, :])
                last.then_inc(s_tr, 1)

            def rank_product(k, j):
                pe.wait_ge(s_tev, NPIECE * (k + 1))
                if j == 0:
                    wait(pe, s_init, k)
                elif j == 1:
                    wait(pe, s_rev, NB * k)
                else:
                    pe.wait_ge(s_rev, NB * k + j - 1)
                for i in range(min(j + 1, NB)):
                    last = pe.matmul(rk_ps[j % 2][:, :], (rank_mat if i == j else ones)[:, :], mask_t[:, i, :],
                                     start=(i == 0), stop=(i == min(j, NB - 1)))
                last.then_inc(s_rk, 1)

            def slot_product(k, h, s):
                if s == 0:
                    pe.wait_ge(s_parts, k + 1)
                pe.wait_ge(s_oh, S * k + s + 1)
                wait(pe, s_max, S * k + s - NRING + 1)
                r = (S * h + s) % NRING
                for j in range(NB):
                    for part_ in range(2):
                        last = pe.matmul(bank[r][:, :], xparts[:, h, j, part_, :], onehot[:, r, j * CH:(j + 1) * CH],
                                         start=(j == 0 and part_ == 0), stop=(j == NB - 1 and part_ == 1))
                last.then_inc(s_slot, 1)

            def transpose_xs(k, b, h):
                pe.wait_ge(s_lgd, k + 1)
                if h == 0:
                    pe.wait_ge(s_routed, b + 1)
                for i in range(CT):
                    last = pe.transpose(fin_ps[:, i * P:(i + 1) * P], xs[:, h, CT * h + i, :], ident32[:, :])
                last.then_inc(s_xt, 1)

            def transpose_near(k):
                pe.wait_ge(s_xtev, k + 1)
                pe.wait_ge(s_red, CT * (k + 1))
                for i in range(CT):
                    last = pe.transpose(fin_ps[:, i * P:(i + 1) * P], near_max[:, i, :], ident32[:, :])
                last.then_inc(s_nt, 1)

            def gnn_product(k, h):
                pe.wait_ge(s_agg, k + 1)
                for i in range(CT):
                    pe.matmul(fin_ps[:, i * P:(i + 1) * P], xs_t[:, i * P:(i + 1) * P], w_gnn[:, 0, :], start=True, stop=False)
                    last = pe.matmul(fin_ps[:, i * P:(i + 1) * P], agg[:, h, i * P:(i + 1) * P], w_gnn[:, 1, :],
                                     start=False, stop=True)
                last.then_inc(s_fin, 1)

            def transpose_x2(k, h):
                pe.wait_ge(s_pay, k + 1)
                for i in range(CT):
                    last = pe.transpose(fin_ps[:, i * P:(i + 1) * P], pay[:, 0, h, i, 0:C], ident32[:, :])
                last.then_inc(s_x2t, 1)

            def logit_product(k):
                pe.wait_ge(s_x2tev, k + 1)
                for i in range(CT):
                    last = pe.matmul(fin_ps[:, i * NE:(i + 1) * NE], x2_t[:, i * P:(i + 1) * P], gw[:, :], start=True, stop=True)
                last.then_inc(s_lg, 1)

            def route_product(b):
                pe.wait_ge(s_sel, b + 1)
                pe.matmul(fin_ps[:, 0:NB * NE], tri[:, :], sel16[:, :, :].rearrange("p t e -> p (t e)"),
                          start=True, stop=False, skip_group_check=True)
                for t in range(NB - 1):
                    pe.matmul(fin_ps[:, (t + 1) * NE:NB * NE], ones[:, :],
                              sel16[:, t, :].unsqueeze(1).broadcast_to([P, NB - 1 - t, NE]),
                              start=False, stop=False, skip_group_check=True)
                for t in range(NB):
                    last = pe.matmul(fin_ps[:, NB * NE:NB * NE + NE], ones[:, :], sel16[:, t, :],
                                     start=False, stop=(t == NB - 1), skip_group_check=True)
                last.then_inc(s_route, 1)

            def slots(k, b, h, prep, fin):
                fb = b if h else b - 1
                for s in range(S):
                    if fin and s == 1:
                        transpose_xs(k - 1, fb, 1 - h)
                    if fin and s == 2:
                        transpose_near(k - 1)
                    if prep and 2 <= s < 2 + NPIECE:
                        transpose_score(k + 1, s - 2)
                    if fin and s == 4:
                        gnn_product(k - 1, 1 - h)
                    if prep and 6 <= s < 6 + NB // 2:
                        rank_product(k + 1, 2 * (s - 6))
                        rank_product(k + 1, 2 * (s - 6) + 1)
                    if prep and s == 6 + NB // 2:
                        rank_product(k + 1, NB)
                    if fin and s == 7:
                        transpose_x2(k - 1, 1 - h)
                    if fin and s == 8:
                        logit_product(k - 1)
                    if fin and h == 0 and s == 11:
                        route_product(fb)
                    slot_product(k, h, s)

            pe.wait_ge(s_const, N_CONST)
            pe.wait_ge(s_w, 64)
            for q in range(NPIECE):
                transpose_score(0, q)
            for j in range(NB + 1):
                rank_product(0, j)
            chunks(pe, slots)
            transpose_xs(NCHUNK - 1, B - 1, 1)
            transpose_near(NCHUNK - 1)
            gnn_product(NCHUNK - 1, 1)
            transpose_x2(NCHUNK - 1, 1)
            logit_product(NCHUNK - 1)
            route_product(B - 1)

            def transpose_rows(j, u, turn):
                pe.wait_ge(s_xd[u % UN], 16 * (turn + 1 + u // UN))
                wait(pe, s_xdtev, j - 1)
                pe.transpose(bank[u % 2][:, 0:P], xd[:, u % UN, 0:C], ident32[:, :]).then_inc(s_xdt, 1)

            def expert_of(j):
                return pe.value_load(tile_i[0:1, 0, ds(j, 1)], min_val=0, max_val=NE - 1)

            def hidden_product(j, u, e):
                pe.wait_ge(s_xdtev, j + 1)
                wait(pe, s_hid, j - 1)
                pe.matmul(bank[2 + u % 2][:, :], xd_t[:, u % 2, :], w12[:, ds(e, 1), :].rearrange("p a h -> p (a h)"),
                          start=True, stop=True).then_inc(s_h, 1)

            def transpose_hidden(j, u):
                pe.wait_ge(s_hid, j + 1)
                wait(pe, s_htev, j)
                for c in range(2):
                    last = pe.transpose(hid_t_ps[:, c * P:(c + 1) * P], hid[:, u % 2, c * P:(c + 1) * P], ident32[:, :])
                last.then_inc(s_ht, 1)

            def output_product(j, u, e):
                pe.wait_ge(s_htev, j + 1)
                wait(pe, s_yev, j - 1)
                for c in range(2):
                    last = pe.matmul(y_ps[u % 2][:, 0:P], hid_t[:, u % 2, c * P:(c + 1) * P],
                                     w3_sb[:, ds(e, 1), c, :].rearrange("p a o -> p (a o)"), start=(c == 0), stop=(c == 1))
                last.then_inc(s_y, 1)

            def tiles(j0, turn, left):
                opening = isinstance(j0, int) and j0 == 0
                before = None if opening else expert_of(j0 - 1)
                here = expert_of(j0)
                after = expert_of(j0 + 1)
                for u in range(UN):
                    j = j0 + u
                    if u + 1 < left:
                        hidden_product(j + 1, u + 1, after)
                    if u < UN - 1 and u + 2 < left:
                        coming = expert_of(j + 2)
                    if before is not None:
                        output_product(j - 1, u + 1, before)
                    transpose_hidden(j, u)
                    if u + 3 < left:
                        transpose_rows(j + 3, u + 3, turn)
                    before, here, after = here, after, coming

            pe.wait_ge(s_map, 1)
            pe.wait_ge(s_wexp, 64)
            transpose_rows(0, 0, 0)
            transpose_rows(1, 1, 0)
            hidden_product(0, 0, expert_of(0))
            transpose_rows(2, 2, 0)
            expert_turns(pe, tiles)
            output_product(PAIR_TILES - 1, UN - 1, expert_of(PAIR_TILES - 1))


def kernel(**inputs):
    import numpy as _np
    import concourse.bacc as _bacc
    from concourse import mybir as _mybir
    from concourse.bass_utils import run_bass_kernel_spmd as _run

    names = ["x", "adj", "L0_gnn_W", "L0_gnn_b", "L0_ffn_gate_w", "L0_ffn_gate_b", "L0_ffn_w1", "L0_ffn_w2", "L0_ffn_w3"]
    nc = _bacc.Bacc("TRN2", target_bir_lowering=False, num_devices=1)
    arrays, args = {}, []
    for name in names:
        a = _np.ascontiguousarray(inputs[name])
        arrays[f"in_{name}"] = a
        args.append(nc.dram_tensor(f"in_{name}", a.shape, _mybir.dt.from_np(a.dtype), kind="ExternalInput").ap())
    shape = inputs["x"].shape
    args.append(nc.dram_tensor("out_0", shape, _mybir.dt.float32, kind="ExternalOutput").ap())
    build(nc, *args)
    r = _run(nc, [arrays], core_ids=[0])
    return r.results[0]["out_0"]
```

```python
import concourse.bass as bass
from concourse import mybir
from contextlib import ExitStack
import numpy as np


def build(nc, x, adj, W, bias, gate_w, gate_b, w1, w2, w3, out):
    f32, f16, i32, u32 = mybir.dt.float32, mybir.dt.float16, mybir.dt.int32, mybir.dt.uint32
    ALU = mybir.AluOpType
    ACT = mybir.ActivationFunctionType
    AX = mybir.AxisListType
    ds = bass.ds

    P = 128
    B, N, C = x.shape
    NE, _, HID = w1.shape
    NB = N // P
    CH = 512
    CT = CH // P
    HALVES = N // CH
    NCHUNK = B * HALVES
    TILES = B * NB
    NEIGH = 25
    SG = 11
    S = NEIGH - SG
    MORE = (3, 3)
    LIGHT = 6
    SHIFT = 64
    PIECE = 2
    NPIECE = NB // PIECE
    NRING = 4
    ACT_SLOTS = (1, 13)
    assert LIGHT not in ACT_SLOTS and 0 not in ACT_SLOTS
    ACT_N, DVE_N = len(ACT_SLOTS), S - len(ACT_SLOTS)
    REDUCED = ((5, 7, 10, 13), (5, 7, 9, 13))
    EPS = 1e-5
    SCALE = 4096.0
    assert SCALE * np.sqrt(C - 1) < 65504 and NEIGH < SHIFT and HALVES == 2 and 8 < SG <= 16
    assert HALVES * S % NRING == 0 and S == 14
    BIG = 3.0e38
    PAIR_TILES = TILES * 2 + NE
    KNOWN = ((B - 1) * N * 2 - NE * (P - 1)) // P
    REST = PAIR_TILES - KNOWN
    MAPPED = 48
    UN = 12
    TURNS = PAIR_TILES // UN
    assert PAIR_TILES % UN == 0 and KNOWN % UN == 0 and KNOWN % MAPPED == 0 and REST == MAPPED
    TOKENS = TILES * P
    REGION = TOKENS + P
    PW = C + 1
    PAIRS = 2 * TOKENS
    FILL = NE * P

    x_rows = x.rearrange("b n c -> (b n) c")
    adj_rows = adj.rearrange("b n m -> (b n) m")
    out_rows = out.rearrange("b n c -> (b n) c")
    FEAT = N + 1
    feat = nc.dram_tensor("feat", (B * FEAT, C), f32).ap()
    dispatched = nc.dram_tensor("dispatched", (NE * REGION + FILL, PW), f32).ap()
    pair_rows = nc.dram_tensor("pair_rows", (PAIRS + 2 * FILL, C), f32).ap()

    ctx = ExitStack()
    with ctx:
        def sb(name, shape, dt):
            return ctx.enter_context(nc.sbuf_tensor(name, shape, dt))

        def sem(name):
            return ctx.enter_context(nc.semaphore(name))

        x1 = sb("x1", [P, TILES, C], f32)
        adj_in = sb("adj_in", [P, CT, N], i32)
        shared = sb("shared", [P, 4, NB * CH], f16)
        score = shared[:, 0, :].rearrange("p (t n) -> p t n", t=CT)
        score2 = shared[:, 1, :].rearrange("p (t n) -> p t n", t=CT)
        mask_t = shared[:, 2, :].rearrange("p (j c) -> p j c", j=NB)
        rank_t = (shared[:, 3, :], sb("rank_t", [P, NB * CH], f16)[:, :])
        falling = sb("falling", [P, N], f16)
        first = sb("first", [P, CT, 16], f16)
        nb_row = sb("nb_row", [P, 2, CT, 16], i32)
        feat_end = sb("feat_end", [P, 1], f32)
        near = sb("near", [P, CT, SG + 1, C], f32)
        near_max = sb("near_max", [P, CT, C], f32)
        onehot = sb("onehot", [P, NRING, NB * CH], f16)
        xparts = sb("xparts", [P, 2, NB, 2, C], f16)
        xin = sb("xin", [P, NB, C], f32)
        xin_2 = sb("xin_2", [P, CT, C], f32)
        xs = sb("xs", [P, NB, C], f32)
        xs_2 = sb("xs_2", [P, CT, C], f32)
        agg = sb("agg", [P, 2, CH], f32)
        xs_t = sb("xs_t", [P, CH], f32)
        gnn_tmp = sb("gnn_tmp", [P, CT, C], f32)
        pay = sb("pay", [P, 2, 2, CT, PW], f32)
        x2_t = xs_t
        fill = sb("fill", [P, NE, PW], f32)
        stats1 = sb("stats1", [P, NB, 6], f32)
        mv1 = sb("mv1", [P, NB, 2], f32)
        std1 = sb("std1", [P, 3, NB], f32)
        stats2 = sb("stats2", [P, CT, 6], f32)
        mv2 = sb("mv2", [P, CT, 2], f32)
        std2 = sb("std2", [P, 3, CT], f32)
        w_gnn = sb("w_gnn", [P, 2, C], f32)
        bias_bc = sb("bias_bc", [P, C], f32)
        gw = sb("gw", [P, NE], f32)
        gb_bc = sb("gb_bc", [P, NE], f32)
        ident16 = sb("ident16", [P, P], f16)
        ident32 = sb("ident32", [P, P], f32)
        rank_mat = sb("rank_mat", [P, P], f16)
        rank_next = sb("rank_next", [P, P], f16)
        tri = sb("tri", [P, P], f16)
        ones = sb("ones", [P, P], f16)
        slot_bias = sb("slot_bias", [P, S], f32)
        one = sb("one", [P, 1], f32)
        iota_m = sb("iota_m", [P, NE], f32)
        region = sb("region", [P, NE], f32)
        logits = sb("logits", [P, NB, NE], f32)
        lmask = sb("lmask", [P, NB, NE], f32)
        eqi = sb("eqi", [P, NB, NE], f32)
        oh = sb("oh", [P, 2, NB, NE], f32)
        pos_e = sb("pos_e", [P, NB, NE], f32)
        best = sb("best", [P, 4, NB], f32)
        pos_f = sb("pos_f", [P, 2, NB], f32)
        pos_i = sb("pos_i", [P, 2, NB], i32)
        sel16 = sb("sel16", [P, NB, NE], f16)
        taken = sb("taken", [P, NE], f32)
        gap = sb("gap", [P, TILES], f32)
        gap_exp = sb("gap_exp", [P, TILES], f32)
        weight = sb("weight", [P, 3, TILES], f32)
        w12 = shared[:, :, :].rearrange("p r f -> p (r f)").bitcast(f32).rearrange("p (e h) -> p e h", e=NE)
        w3_sb = adj_in[:, :, :].rearrange("p t n -> p (t n)").bitcast(f32).rearrange("p (e k o) -> p e k o", e=NE, k=2)
        cnt_i = sb("cnt_i", [P, 3, NE], i32)
        count = sb("count", [P, NE], f32)
        full = sb("full", [P, NE], f32)
        all_t = sb("all_t", [P, NE], f32)
        done_t = sb("done_t", [P, NE + 1], f32)
        left_t = sb("left_t", [P, NE], f32)
        upto = sb("upto", [P, NE], f32)
        step = sb("step", [P, NE], f32)
        one_e = sb("one_e", [P, NE], f32)
        first_row = sb("first_row", [P, 1], f32)
        cnt_fill = cnt_i[:, 2, :]
        nr = near[:, :, :, :].rearrange("p a b c -> p (a b c)")
        tile_no = sb("tile_no", [P, PAIR_TILES], f32)
        tile_row = sb("tile_row", [P, MAPPED * 2], f32)
        tile_f = sb("tile_f", [P, 2, MAPPED], f32)
        tile_i = sb("tile_i", [P, 2, PAIR_TILES], i32)
        w_tile = xs[:, :, :].rearrange("p t c -> p (t c)").rearrange("p (r h) -> p r h", r=2)
        words = onehot[:, :, :].rearrange("p r f -> p (r f)").bitcast(f32)
        at = [0]

        def part_of(*shape):
            size = int(np.prod(shape))
            v = words[:, at[0]:at[0] + size]
            at[0] += size
            return v

        silu = part_of(2, HID).rearrange("p (r h) -> p r h", r=2)
        hid_t = part_of(2, HID).rearrange("p (r h) -> p r h", r=2)
        xd_t = part_of(2, P).rearrange("p (r c) -> p r c", r=2)
        xd = part_of(UN, PW).rearrange("p (r c) -> p r c", r=UN)
        yd = part_of(UN, C).rearrange("p (r c) -> p r c", r=UN)
        pair_i = sb("pair_i", [P, UN], i32)
        QT = 4
        GB = 5
        pairs_in = nr[:, 0:GB * QT * 2 * C].rearrange("p (g t c) -> p g t c", g=GB, t=QT)
        res = part_of(GB, QT, C).rearrange("p (g t c) -> p g t c", g=GB, t=QT)

        bank = [ctx.enter_context(nc.psum_tensor(f"slot{i}", [P, CH], f32)) for i in range(NRING)]
        tr_ps = ctx.enter_context(nc.psum_tensor("tr_ps", [P, PIECE, CH], f16))
        rk_ps = [ctx.enter_context(nc.psum_tensor(f"rk_ps{i}", [P, CH], f32)) for i in range(2)]
        fin_ps = ctx.enter_context(nc.psum_tensor("fin_ps", [P, CH], f32))
        y_ps = (rk_ps[1], fin_ps)

        s_w = sem("weights_loaded")
        s_const = sem("constants_ready")
        s_absent = sem("absent_rows_stored")
        s_fill = sem("fill_stored")
        s_adj = [sem(f"adj_loaded{i}") for i in range(CT)]
        s_x = [sem(f"x_loaded{i}") for i in range(2)]
        s_feat = sem("features_stored")
        s_score = sem("score_done")
        s_top = sem("top_chain")
        s_row = sem("neighbour_rows_ready")
        s_near = [sem(f"gathered{i}") for i in range(CT)]
        s_red = sem("near_max_done")
        s_tr = sem("score_transposed")
        s_tev = sem("mask_t_done")
        s_rk = sem("rank_product_done")
        s_rev = sem("rank_t_done")
        s_init = sem("agg_started")
        s_oh = sem("onehot_done")
        s_dist = sem("rank_distance_done")
        s_oha = sem("act_onehot_done")
        s_slot = sem("slot_product_done")
        s_max = sem("max_done")
        s_ln1 = sem("ln1_chain")
        s_std1 = sem("std1_done")
        s_hi = sem("hi_part_done")
        s_parts = sem("x_parts_done")
        s_xt = sem("xs_transposed")
        s_xtev = sem("xs_t_done")
        s_nt = sem("near_max_transposed")
        s_agg = sem("agg_complete")
        s_fin = sem("gnn_product_done")
        s_tmp = sem("gnn_tmp_done")
        s_x1 = sem("x1_done")
        s_ln2 = sem("ln2_chain")
        s_std2 = sem("std2_done")
        s_pay = sem("pay_first_done")
        s_pay2 = sem("pay_second_done")
        s_x2t = sem("x2_transposed")
        s_x2tev = sem("x2_t_done")
        s_lg = sem("logit_product_done")
        s_lgd = sem("logits_done")
        s_rc = sem("routing_chain")
        s_sel = sem("sel_ready")
        s_route = sem("route_product_done")
        s_routed = sem("route_product_read")
        s_pos = sem("positions_ready")
        s_scat = sem("scattered")
        s_sent = sem("batch_scattered")
        s_cc = sem("counting_chain")
        s_exp = sem("exp_done")
        s_wexp = sem("expert_weights_loaded")
        s_filled = sem("tiles_filled")
        s_map = sem("tile_map_ready")
        s_falling = sem("falling_ready")
        s_numbered = sem("filling_numbered")
        s_fe = sem("feat_end_ready")
        s_filled_at = sem("filling_rows_known")
        s_gaps = sem("gap_written")
        s_share = sem("shares_chain")
        s_xd = [sem(f"rows_loaded{i}") for i in range(UN)]
        s_xdt = sem("rows_transposed")
        s_xdtev = sem("rows_t_done")
        s_pid = sem("pair_number_done")
        s_h = sem("hidden_product_done")
        s_silu = sem("silu_done")
        s_hid = sem("hidden_done")
        s_wt = sem("tile_weights_copied")
        s_y = sem("expert_product_done")
        s_yev = sem("expert_rows_ready")
        s_yst = [sem(f"expert_rows_scattered{i}") for i in range(UN)]
        s_g = [sem(f"pairs_loaded{i}") for i in range(GB)]
        s_c1 = sem("combine_first")
        s_res = sem("result_ready")
        s_out = [sem(f"out_stored{i}") for i in range(GB)]

        def wait(eng, s, value):
            if not (isinstance(value, int) and value <= 0):
                eng.wait_ge(s, value)

        def chunks(eng, slots):
            slots(0, 0, 0, True, False)
            with eng.Fori(0, B - 1) as b:
                slots(2 * b + 1, b, 1, True, True)
                slots(2 * b + 2, b + 1, 0, True, True)
            slots(NCHUNK - 1, B - 1, 1, False, True)

        def expert_turns(eng, tiles):
            tiles(0, 0, 2 * UN)
            tiles(UN, 1, 2 * UN)
            with eng.Fori(2, TURNS - 1) as i:
                tiles(UN * i, i, 2 * UN)
            tiles(PAIR_TILES - UN, TURNS - 1, UN)

        def act_count(k, s):
            return ACT_N * k + len([a for a in ACT_SLOTS if a < s])

        def dve_count(k, s):
            return DVE_N * k + len([a for a in range(s) if a not in ACT_SLOTS])

        def slot_start(h, s):
            return MORE[h] * P if s == LIGHT else 0

        def rank_of(s):
            return SG + {0: LIGHT, LIGHT: 0}.get(s, s)

        def gathers(h, i):
            return SG + (1 if i < MORE[h] else 0)

        def gathered(b, h, i):
            return (gathers(0, i) + gathers(1, i)) * b + gathers(0, i) + (gathers(1, i) if h else 0)

        N_CONST = 23
        LN1_VAR, LN1 = 3, 5
        LN2_VAR, LN2 = 3, 4
        TOP = 3
        RC_A, RC_B = 11, 6
        RC = RC_A + RC_B

        block = ctx.enter_context(nc.Block())

        @block.sync
        def _(sp):
            def load_x(k, b, h):
                wait(sp, s_x1, k - 1)
                if h == 0:
                    sp.dma_start(xin[:, :, :], x_rows[ds(b * N, N), :].rearrange("(t p) c -> p t c", p=P))\
                        .then_inc(s_x[0], 16)
                else:
                    sp.dma_start(xin_2[:, :, :], x_rows[ds(b * N + CH, CH), :].rearrange("(t p) c -> p t c", p=P))\
                        .then_inc(s_x[1], 16)

            def load_adj(k, i):
                wait(sp, s_score, CT * (k - 1) + i + 1)
                sp.dma_start(adj_in[:, i, :], adj_rows[ds(k * CH + i * P, P), :]).then_inc(s_adj[i], 16)

            def store_features(b):
                sp.wait_ge(s_ln1, LN1 * (b + 1))
                sp.dma_start(feat[ds(b * FEAT, N), :].rearrange("(t p) c -> p t c", p=P), xs[:, :, :])\
                    .then_inc(s_feat, 16)

            load_adj(0, 0)
            load_x(0, 0, 0)
            for i in range(1, CT):
                load_adj(0, i)
            sp.dma_start(w_gnn[:, :, :], W.rearrange("(k p) o -> p k o", p=P)).then_inc(s_w, 16)
            sp.dma_start(bias_bc[:, :], bias.rearrange("(a o) -> a o", a=1).broadcast_to([P, C])).then_inc(s_w, 16)
            sp.dma_start(gw[:, :], gate_w).then_inc(s_w, 16)
            sp.dma_start(gb_bc[:, :], gate_b.rearrange("(a o) -> a o", a=1).broadcast_to([P, NE])).then_inc(s_w, 16)
            sp.wait_ge(s_const, N_CONST)
            for i in range(B * N // FILL):
                sp.dma_start(feat[i * FILL:(i + 1) * FILL, :].rearrange("(e p) c -> p e c", p=P),
                             fill[:, :, 0:C]).then_inc(s_absent, 16)
            sp.dma_start(feat[B * N:B * FEAT, :], fill[0:B, 0, 0:C]).then_inc(s_absent, 16)
            sp.wait_ge(s_absent, 16 * (B * N // FILL + 1))
            store_features(0)
            for i in range(CT):
                load_adj(1, i)
            load_x(1, 0, 1)
            sp.dma_start(dispatched[NE * REGION:NE * REGION + FILL, :].rearrange("(e p) c -> p e c", p=P),
                         fill[:, :, :]).then_inc(s_fill, 16)
            with sp.Fori(0, B - 1) as b:
                for i in range(CT):
                    load_adj(2 * b + 2, i)
                load_x(2 * b + 2, b + 1, 0)
                store_features(b + 1)
                for i in range(CT):
                    load_adj(2 * b + 3, i)
                load_x(2 * b + 3, b + 1, 1)

            sp.wait_ge(s_score, CT * NCHUNK)
            for k in range(2):
                sp.dma_start(w3_sb[:, :, k, :], w3[:, k * P:(k + 1) * P, :].rearrange("e h o -> h e o"))\
                    .then_inc(s_wexp, 16)
            sp.wait_ge(s_tr, NPIECE * NCHUNK)
            sp.wait_ge(s_top, TOP * NCHUNK)
            sp.wait_ge(s_rk, (NB + 1) * NCHUNK)
            sp.wait_ge(s_oh, dve_count(NCHUNK - 1, 0))
            sp.wait_ge(s_dist, act_count(NCHUNK - 1, 0))
            sp.dma_start(w12[:, :, 0:HID], w1.rearrange("e d h -> d e h")).then_inc(s_wexp, 16)
            sp.dma_start(w12[:, :, HID:2 * HID], w2.rearrange("e d h -> d e h")).then_inc(s_wexp, 16)

            def load_rows(j, u):
                row = sp.value_load(tile_i[0:1, 1, ds(j, 1)], min_val=0, max_val=NE * REGION + FILL - P)
                wait(sp, s_xdt, j - UN + 1)
                if not isinstance(j, int) or j >= UN:
                    sp.wait_ge(s_pid, j - UN + 1)
                sp.dma_start(xd[:, u, :], dispatched[ds(row, P), :]).then_inc(s_xd[u], 16)

            FILLS = NE // (KNOWN // UN)

            def fill_up(i):
                for c in range(FILLS):
                    row = sp.value_load(cnt_fill[0:1, ds(FILLS * i + c, 1)], min_val=0, max_val=NE * REGION - P)
                    sp.dma_start(dispatched[ds(row, P), :], fill[:, ds(FILLS * i + c, 1), :].rearrange("p a c -> p (a c)"))\
                        .then_inc(s_filled, 16)

            sp.wait_ge(s_map, 1)
            sp.wait_ge(s_scat, 2 * (TILES - NB) * 16)
            sp.wait_ge(s_slot, S * NCHUNK)
            for u in range(UN):
                load_rows(u, u)
            sp.wait_ge(s_filled_at, 1)
            sp.wait_ge(s_numbered, 1)
            fill_up(0)
            with sp.Fori(1, KNOWN // UN) as i:
                for u in range(UN):
                    load_rows(UN * i + u, u)
                fill_up(i)
            sp.wait_ge(s_map, 2)
            sp.wait_ge(s_filled, NE * 16)
            sp.wait_ge(s_scat, 2 * TILES * 16)
            sp.wait_ge(s_fill, 16)
            with sp.Fori(KNOWN // UN, TURNS) as i:
                for u in range(UN):
                    load_rows(UN * i + u, u)

            for u in range(UN):
                sp.wait_ge(s_yst[u], 16 * TURNS)
            quads = TILES // QT

            def load_pairs(q):
                if q >= GB:
                    sp.wait_ge(s_res, QT * (q - GB + 1))
                sp.dma_start(pairs_in[:, q % GB, :, :],
                             pair_rows[2 * q * QT * P:2 * (q + 1) * QT * P, :].rearrange("(t p c) d -> p t (c d)", p=P, c=2))\
                    .then_inc(s_g[q % GB], 16)

            for q in range(quads):
                load_pairs(q)

        @block.gpsimd
        def _(pool):
            pool.sem_inc(s_sent, 1)
            n = [0]

            def done(ins):
                n[0] += 1
                ins.then_inc(s_const, 1)

            def iota(ap, pattern, base, channel_multiplier):
                done(pool.iota(ap, pattern=pattern, base=base, channel_multiplier=channel_multiplier,
                               allow_small_or_imprecise_dtypes=True))

            pool.iota(falling[:, :], pattern=[[-1, N]], base=N, channel_multiplier=0,
                      allow_small_or_imprecise_dtypes=True).then_inc(s_falling, 1)
            done(pool.memset(ident16[:, :], 0.0))
            done(pool.memset(ident32[:, :], 0.0))
            done(pool.memset(rank_mat[:, :], 1.0))
            done(pool.memset(rank_next[:, :], 1.0))
            done(pool.memset(tri[:, :], 1.0))
            done(pool.memset(ones[:, :], 1.0))
            pool.wait_ge(s_const, n[0])
            for m in (ident16, ident32):
                done(pool.affine_select(out=m[:, :], in_=m[:, :], compare_op=ALU.not_equal, fill=1.0, base=0,
                                        pattern=[[-1, P]], channel_multiplier=1))
            for m in (rank_mat, tri):
                done(pool.affine_select(out=m[:, :], in_=m[:, :], compare_op=ALU.is_gt, fill=0.0, base=0,
                                        pattern=[[1, P]], channel_multiplier=-1))
            done(pool.affine_select(out=rank_next[:, :], in_=rank_next[:, :], compare_op=ALU.is_ge, fill=0.0, base=0,
                                    pattern=[[-1, P]], channel_multiplier=1))
            pool.wait_ge(s_const, n[0])
            done(pool.affine_select(out=rank_next[:, :], in_=rank_next[:, :], compare_op=ALU.not_equal,
                                    fill=1.0 + SHIFT, base=0, pattern=[[-1, P]], channel_multiplier=1))
            done(pool.affine_select(out=rank_mat[:, :], in_=rank_mat[:, :], compare_op=ALU.not_equal,
                                    fill=-float(SHIFT), base=0, pattern=[[-1, P]], channel_multiplier=1))
            iota(slot_bias[:, :], [[-1, S]], SHIFT - SG, 0)
            done(pool.memset(one[:, :], 1.0))
            iota(iota_m[:, :], [[1, NE]], -64, 0)
            iota(region[:, :], [[REGION, NE]], 0, 0)
            iota(tile_no[:, :], [[1, PAIR_TILES]], 0, 0)
            iota(tile_row[:, :], [[P, 2 * MAPPED]], 0, 0)
            for h in range(2):
                iota(pay[:, :, h, :, C], [[1, 2], [2 * P, CT]], 2 * CH * h - 2 * N, 2)
            done(pool.memset(fill[:, :, 0:C], 0.0))
            iota(fill[:, :, C], [[P, NE]], PAIRS + FILL, 1)

            def gather(k, h, i, columns=None):
                if columns is None:
                    columns = range(gathers(h, i))
                if i == 0:
                    pool.wait_ge(s_row, k + 1)
                if columns[0] == 0:
                    wait(pool, s_red, CT * (k - 1) + i + 1)
                    pool.nop(nofuse=True)
                for c in columns:
                    pool.indirect_dma_start(
                        out=near[:, i, c, :], out_offset=None, in_=feat[:, :],
                        in_offset=bass.IndirectOffsetOnAxis(ap=nb_row[:, h, i, c:c + 1].bitcast(u32), axis=0))\
                        .then_inc(s_near[i], 16)

            def scatter(b):
                pool.wait_ge(s_pos, b + 1)
                pool.wait_ge(s_pay2, 2 * (b + 1))
                pool.nop(nofuse=True)
                for t in range(NB):
                    for c in range(2):
                        pool.indirect_dma_start(
                            out=dispatched[:, :], out_offset=bass.IndirectOffsetOnAxis(ap=pos_i[:, c, t:t + 1].bitcast(u32), axis=0),
                            in_=pay[:, c, t // CT, t % CT, :], in_offset=None).then_inc(s_scat, 16)

            BEGUN = 3

            def slots(k, b, h, prep, fin):
                if h == 0:
                    pool.wait_ge(s_feat, 16 * (b + 1))
                    pool.nop(nofuse=True)
                if h:
                    gather(k, h, 1, range(BEGUN, gathers(h, 1)))
                    gather(k, h, 2)
                    gather(k, h, 3)
                else:
                    for i in range(CT):
                        gather(k, h, i)
                    gather(k + 1, 1, 0)
                    if fin:
                        scatter(b - 1)
                    gather(k + 1, 1, 1, range(BEGUN))
                    if fin:
                        pool.wait_ge(s_scat, 16 * 2 * NB * b)
                        pool.sem_inc(s_sent, 1)

            assert n[0] == N_CONST
            pool.wait_ge(s_absent, 16 * (B * N // FILL + 1))
            chunks(pool, slots)
            pool.wait_ge(s_fill, 16)
            pool.tensor_scalar(fill[:, :, C], fill[:, :, C], 1.0, -float(FILL), ALU.mult, ALU.add).then_inc(s_numbered, 1)
            scatter(B - 1)

            def pair_numbers(j, u, turn):
                pool.wait_ge(s_xd[u], 16 * (turn + 1))
                wait(pool, s_yst[u], 16 * turn)
                pool.nop(nofuse=True)
                pool.tensor_copy(pair_i[:, u:u + 1], xd[:, u, C:C + 1]).then_inc(s_pid, 1)

            def tiles(j0, turn, left):
                for u in range(UN):
                    if u + 1 < left:
                        pair_numbers(j0 + u + 1, (u + 1) % UN, turn + (u + 1) // UN)
                    pool.wait_ge(s_pid, j0 + u + 1)
                    pool.wait_ge(s_yev, j0 + u + 1)
                    pool.nop(nofuse=True)
                    pool.indirect_dma_start(
                        out=pair_rows[:, :], out_offset=bass.IndirectOffsetOnAxis(ap=pair_i[:, u:u + 1].bitcast(u32), axis=0),
                        in_=yd[:, u, :], in_offset=None).then_inc(s_yst[u], 16)

            pair_numbers(0, 0, 0)
            expert_turns(pool, tiles)

        @block.scalar
        def _(act):
            def evac_mask(k, q):
                act.wait_ge(s_tr, NPIECE * k + q + 1)
                if q == 0:
                    wait(act, s_rk, (NB + 1) * k)
                act.activation(mask_t[:, PIECE * q:PIECE * (q + 1), :], tr_ps[:, :, :], ACT.Sign).then_inc(s_tev, 1)

            def evac_rank(k, h, n):
                j = n // 2 + NB // 2 * (n % 2)
                act.wait_ge(s_rk, (NB + 1) * k + n + 1)
                if n == 0:
                    wait(act, s_oh, dve_count(k - 1, 0))
                    wait(act, s_dist, act_count(k - 1, 0))
                act.activation(rank_t[h][:, j * CH:(j + 1) * CH], rk_ps[n % 2][:, :], ACT.Copy).then_inc(s_rev, 1)

            def make_onehot(k, h, s):
                act.wait_ge(s_rev, NB * (k + 1))
                wait(act, s_slot, S * k + s - NRING + 1)
                buf = onehot[:, (S * h + s) % NRING, :]
                act.activation(buf, rank_t[h], ACT.Abs,
                               bias=slot_bias[:, s:s + 1]).then_inc(s_dist, 1)
                act.wait_ge(s_dist, act_count(k, s) + 1)
                act.activation(buf, buf, ACT.Relu, bias=one[:, 0:1], scale=-1.0).then_inc(s_oha, 1)

            def root1(b):
                act.wait_ge(s_ln1, LN1 * b + LN1_VAR)
                act.activation(std1[:, 1, :], std1[:, 0, :], ACT.Sqrt).then_inc(s_std1, 1)

            def hi_part(k, b):
                act.wait_ge(s_ln1, LN1 * (b + 1))
                wait(act, s_slot, S * (k - 1))
                act.activation(xparts[:, 0, :, 0, :], xs[:, :, :], ACT.Copy).then_inc(s_hi, 1)

            def second_chunk(k):
                act.wait_ge(s_parts, k)
                wait(act, s_slot, S * (k - 1))
                act.activation(xparts[:, 1, :, :, :], xparts[:, 0, :, :, :], ACT.Copy)
                wait(act, s_xt, k - 1)
                act.activation(xs_2[:, :, :], xs[:, CT:NB, :], ACT.Copy).then_inc(s_parts, 1)

            def evac_xs(k):
                act.wait_ge(s_xt, k + 1)
                act.activation(xs_t[:, :], fin_ps[:, :], ACT.Copy).then_inc(s_xtev, 1)

            def root2(k):
                act.wait_ge(s_ln2, LN2 * k + LN2_VAR)
                act.activation(std2[:, 1, :], std2[:, 0, :], ACT.Sqrt).then_inc(s_std2, 1)

            def second_pay(k, h):
                act.wait_ge(s_pay, k + 1)
                act.activation(pay[:, 1, h, :, 0:C], pay[:, 0, h, :, 0:C], ACT.Copy).then_inc(s_pay2, 1)

            def evac_x2(k):
                act.wait_ge(s_x2t, k + 1)
                act.activation(x2_t[:, :], fin_ps[:, :], ACT.Copy).then_inc(s_x2tev, 1)

            def slots(k, b, h, prep, fin):
                for s in range(S):
                    if fin and s == 1:
                        evac_xs(k - 1)
                    if prep and 2 <= s < 2 + NPIECE:
                        evac_mask(k + 1, s - 2)
                    if fin and s == 5:
                        root2(k - 1)
                    if prep and 6 <= s < 6 + NB // 2:
                        evac_rank(k + 1, 1 - h, 2 * (s - 6))
                        evac_rank(k + 1, 1 - h, 2 * (s - 6) + 1)
                    if fin and s == 7:
                        second_pay(k - 1, 1 - h)
                        evac_x2(k - 1)
                    if prep and h and s == 7:
                        root1(b + 1)
                    if prep and h and s == 9:
                        hi_part(k + 1, b + 1)
                    if prep and not h and s == 9:
                        second_chunk(k + 1)
                    ahead = s + NRING - 1
                    if ahead in ACT_SLOTS:
                        make_onehot(k, h, ahead)
                    elif prep and ahead - S in ACT_SLOTS:
                        make_onehot(k + 1, 1 - h, ahead - S)

            for q in range(NPIECE):
                evac_mask(0, q)
            root1(0)
            hi_part(0, 0)
            for j in range(NB):
                evac_rank(0, 0, j)
            act.wait_ge(s_const, N_CONST)
            for s in range(NRING - 1):
                if s in ACT_SLOTS:
                    make_onehot(0, 0, s)
            chunks(act, slots)
            evac_xs(NCHUNK - 1)
            root2(NCHUNK - 1)
            second_pay(NCHUNK - 1, 1)
            evac_x2(NCHUNK - 1)

            act.wait_ge(s_gaps, B)
            act.activation(gap_exp[:, :], gap[:, :], ACT.Exp).then_inc(s_exp, 1)

            def evac_rows(j, u):
                act.wait_ge(s_xdt, j + 1)
                act.activation(xd_t[:, u % 2, :], bank[u % 2][:, 0:P], ACT.Copy).then_inc(s_xdtev, 1)

            def do_silu(j, u):
                act.wait_ge(s_h, j + 1)
                wait(act, s_hid, j - 1)
                act.activation(silu[:, u % 2, :], bank[2 + u % 2][:, 0:HID], ACT.Silu).then_inc(s_silu, 1)

            def evac_y(j, u, turn):
                act.wait_ge(s_y, j + 1)
                wait(act, s_yst[u], 16 * turn)
                act.activation(yd[:, u, :], y_ps[u % 2][:, 0:P], ACT.Copy).then_inc(s_yev, 1)

            def tiles(j0, turn, left):
                for u in range(UN):
                    j = j0 + u
                    if u + 1 < left:
                        do_silu(j + 1, u + 1)
                    if u or not isinstance(j0, int) or j0:
                        evac_y(j - 1, (u - 1) % UN, turn if u else turn - 1)
                    if u + 3 < left:
                        evac_rows(j + 3, u + 3)

            for u in range(3):
                evac_rows(u, u)
            do_silu(0, 0)
            expert_turns(act, tiles)
            evac_y(PAIR_TILES - 1, UN - 1, TURNS - 1)

            quads = TILES // QT
            for q in range(quads):
                act.wait_ge(s_res, QT * (q + 1))
                act.dma_start(out_rows[q * QT * P:(q + 1) * QT * P, :].rearrange("(t p) c -> p t c", p=P),
                              res[:, q % GB, :, :]).then_inc(s_out[q % GB], 16)
            for g in range(GB):
                act.wait_ge(s_out[g], 16 * len(range(g, quads, GB)))

        @block.vector
        def _(dve):
            def make_score(k, i):
                dve.wait_ge(s_adj[i], 16 * (k + 1))
                if i == 0:
                    wait(dve, s_tr, NPIECE * k)
                dve.scalar_tensor_tensor(out=score[:, i, :], in0=adj_in[:, i, :], scalar=0.0, in1=falling[:, :],
                                         op0=ALU.not_equal, op1=ALU.mult).then_inc(s_score, 1)

            def top_first(k):
                dve.wait_ge(s_score, CT * (k + 1))
                dve.nop(nofuse=True)
                for i in range(CT):
                    last = dve.max(first[:, i, 0:8], score[:, i, :])
                last.then_inc(s_top, 1)

            def top_drop(k, tiles_):
                dve.wait_ge(s_top, TOP * k + 1)
                dve.nop(nofuse=True)
                for i in tiles_:
                    last = dve.match_replace(score2[:, i, :], first[:, i, 0:8], score[:, i, :], 0.0)
                if tiles_[-1] == CT - 1:
                    last.then_inc(s_top, 1)

            def top_second(k):
                dve.wait_ge(s_top, TOP * k + 2)
                dve.nop(nofuse=True)
                for i in range(CT):
                    last = dve.max(first[:, i, 8:16], score2[:, i, :])
                last.then_inc(s_top, 1)

            def neighbour_rows(k, h):
                dve.wait_ge(s_top, TOP * (k + 1))
                if h == 0:
                    dve.tensor_scalar(feat_end[:, :], feat_end[:, :], float(FEAT), None, ALU.add).then_inc(s_fe, 1)
                dve.wait_ge(s_fe, batch_of[0] + 2)
                dve.tensor_scalar(nb_row[:, h, :, :], first[:, :, :], -1.0, feat_end[:, 0:1], ALU.mult, ALU.add)\
                    .then_inc(s_row, 1)

            batch_of = [0]

            def near_reduce(k, b, h, i):
                dve.wait_ge(s_near[i], 16 * gathered(b, h, i))
                if i == 0:
                    wait(dve, s_nt, k)
                dve.tensor_reduce(near_max[:, i, :], near[:, i, 0:gathers(h, i), :].rearrange("p s c -> p c s"), AX.X, ALU.max)\
                    .then_inc(s_red, 1)

            def agg_merge(k, h):
                dve.wait_ge(s_nt, k + 1)
                dve.wait_ge(s_max, S * (k + 1))
                dve.tensor_tensor(agg[:, h, :], fin_ps[:, :], agg[:, h, :], ALU.max).then_inc(s_agg, 1)

            def ln1_stats(k, b):
                dve.wait_ge(s_x[0], 16 * (b + 1))
                dve.nop(nofuse=True)
                for t in range(NB):
                    last = dve.bn_stats(stats1[:, t, :], xin[:, t, :])
                last.then_inc(s_ln1, 1)
                dve.wait_ge(s_ln1, LN1 * b + 1)
                dve.nop(nofuse=True)
                for t in range(NB):
                    last = dve.bn_aggr(mv1[:, t, :], stats1[:, t, :])
                last.then_inc(s_ln1, 1)
                dve.wait_ge(s_ln1, LN1 * b + 2)
                dve.tensor_scalar(std1[:, 0, :], mv1[:, :, 1], EPS, 1.0 / (SCALE * SCALE), ALU.add, ALU.mult)\
                    .then_inc(s_ln1, 1)

            def ln1_apply(k, b):
                dve.wait_ge(s_std1, b + 1)
                dve.reciprocal(std1[:, 2, :], std1[:, 1, :]).then_inc(s_ln1, 1)
                dve.wait_ge(s_ln1, LN1 * b + LN1_VAR + 1)
                wait(dve, s_xt, k - 1)
                wait(dve, s_parts, k)
                wait(dve, s_feat, 16 * b)
                for t in range(NB):
                    last = dve.tensor_scalar(xs[:, t, :], xin[:, t, :], mv1[:, t, 0:1], std1[:, 2, t:t + 1],
                                             ALU.subtract, ALU.mult)
                last.then_inc(s_ln1, 1)

            def lo_part(b):
                dve.wait_ge(s_hi, b + 1)
                dve.tensor_tensor(xparts[:, 0, :, 1, :], xs[:, :, :], xparts[:, 0, :, 0, :], ALU.subtract)\
                    .then_inc(s_parts, 1)

            def agg_init(k, h):
                dve.wait_ge(s_rk, (NB + 1) * (k + 1))
                wait(dve, s_fin, k - 1)
                dve.tensor_scalar(agg[:, h, :], rk_ps[1][:, :], NEIGH + 0.5, -BIG, ALU.is_gt, ALU.mult).then_inc(s_init, 1)

            def make_onehot(k, h, s):
                if s in ACT_SLOTS:
                    return
                if s == 0:
                    dve.wait_ge(s_rev, NB * (k + 1))
                wait(dve, s_slot, S * k + s - NRING + 1)
                picked, ranks = (v.rearrange("p (j c) -> p j c", j=NB)[:, :, slot_start(h, s):]
                                 for v in (onehot[:, (S * h + s) % NRING, :], rank_t[h]))
                dve.tensor_scalar(picked, ranks, float(rank_of(s) - SHIFT), None, ALU.is_equal).then_inc(s_oh, 1)

            def take_max(k, h, s):
                if s == 0:
                    dve.wait_ge(s_init, k + 1)
                dve.wait_ge(s_slot, S * k + s + 1)
                wait(dve, s_max, S * k + s)
                a = slot_start(h, s)
                dve.tensor_tensor(agg[:, h, a:], bank[(S * h + s) % NRING][:, a:], agg[:, h, a:], ALU.max).then_inc(s_max, 1)

            def gnn_out(k, b, h):
                dve.wait_ge(s_x[h], 16 * (b + 1))
                dve.wait_ge(s_fin, k + 1)
                dve.scalar_tensor_tensor(out=gnn_tmp[:, :, :], in0=fin_ps[:, :].rearrange("p (t c) -> p t c", t=CT),
                                         scalar=1.0 / SCALE, in1=bias_bc[:, :].unsqueeze(1).broadcast_to([P, CT, C]),
                                         op0=ALU.mult, op1=ALU.add).then_inc(s_tmp, 1)
                dve.wait_ge(s_tmp, k + 1)
                dve.scalar_tensor_tensor(out=x1[:, ds(CT * k, CT), :], in0=gnn_tmp[:, :, :], scalar=0.0,
                                         in1=(xin_2[:, :, :] if h else xin[:, 0:CT, :]), op0=ALU.max, op1=ALU.add)\
                    .then_inc(s_x1, 1)

            def ln2_stats(k):
                dve.wait_ge(s_x1, k + 1)
                dve.nop(nofuse=True)
                for t in range(CT):
                    last = dve.bn_stats(stats2[:, t, :], x1[:, CT * k + t, :])
                last.then_inc(s_ln2, 1)
                dve.wait_ge(s_ln2, LN2 * k + 1)
                dve.nop(nofuse=True)
                for t in range(CT):
                    last = dve.bn_aggr(mv2[:, t, :], stats2[:, t, :])
                last.then_inc(s_ln2, 1)
                dve.wait_ge(s_ln2, LN2 * k + 2)
                dve.tensor_scalar(std2[:, 0, :], mv2[:, :, 1], EPS, None, ALU.add).then_inc(s_ln2, 1)

            def ln2_apply(k, b, h):
                dve.wait_ge(s_std2, k + 1)
                dve.reciprocal(std2[:, 2, :], std2[:, 1, :]).then_inc(s_ln2, 1)
                dve.wait_ge(s_sent, b + 1)
                dve.tensor_scalar(pay[:, :, h, :, C], pay[:, :, h, :, C], float(2 * N), None, ALU.add)
                dve.wait_ge(s_ln2, LN2 * (k + 1))
                for t in range(CT):
                    last = dve.tensor_scalar(pay[:, 0, h, t, 0:C], x1[:, CT * k + t, :], mv2[:, t, 0:1],
                                             std2[:, 2, t:t + 1], ALU.subtract, ALU.mult)
                last.then_inc(s_pay, 1)

            def logits_out(k, h):
                dve.wait_ge(s_lg, k + 1)
                dve.tensor_tensor(logits[:, CT * h:CT * h + CT, :], fin_ps[:, 0:CT * NE].rearrange("p (t e) -> p t e", t=CT),
                                  gb_bc[:, :].unsqueeze(1).broadcast_to([P, CT, NE]), ALU.add).then_inc(s_lgd, 1)

            def over_e(v, rows=NB):
                return v.unsqueeze(2).broadcast_to([P, rows, NE])

            def over_t(v, rows=NB):
                return v.unsqueeze(1).broadcast_to([P, rows, NE])

            def chain(semaphore, base, steps):
                n = [0]

                def link(ins=None):
                    if ins is None:
                        assert n[0] == steps, n
                        return
                    n[0] += 1
                    ins.then_inc(semaphore, 1)
                    dve.wait_ge(semaphore, base + n[0])
                return link

            def route_first(b):
                link = chain(s_rc, RC * b, RC_A)
                dve.wait_ge(s_lgd, 2 * b + 3)
                for c, src in enumerate((logits[:, :, :], lmask[:, :, :])):
                    link(dve.tensor_reduce(best[:, c, :], src, AX.X, ALU.max))
                    link(dve.tensor_tensor(eqi[:, :, :], src, over_e(best[:, c, :]), ALU.is_equal))
                    link(dve.tensor_tensor(eqi[:, :, :], eqi[:, :, :], over_t(iota_m[:, :]), ALU.mult))
                    link(dve.tensor_reduce(best[:, 2 + c, :], eqi[:, :, :], AX.X, ALU.min))
                    link(dve.tensor_tensor(oh[:, c, :, :], over_t(iota_m[:, :]), over_e(best[:, 2 + c, :]), ALU.is_equal))
                    if c == 0:
                        link(dve.scalar_tensor_tensor(out=lmask[:, :, :], in0=oh[:, 0, :, :], scalar=-BIG,
                                                      in1=logits[:, :, :], op0=ALU.mult, op1=ALU.add))
                link()
                dve.tensor_tensor(sel16[:, :, :], oh[:, 0, :, :], oh[:, 1, :, :], ALU.add).then_inc(s_sel, 1)
                dve.tensor_tensor(gap[:, ds(NB * b, NB)], best[:, 1, :], best[:, 0, :], ALU.subtract).then_inc(s_gaps, 1)

            def route_second(b):
                link = chain(s_rc, RC * b + RC_A, RC_B)
                dve.wait_ge(s_route, b + 1)
                link(dve.tensor_tensor(pos_e[:, :, :], fin_ps[:, 0:NB * NE].rearrange("p (t e) -> p t e", e=NE),
                                       over_t(taken[:, :]), ALU.add))
                link(dve.tensor_tensor(taken[:, :], fin_ps[:, NB * NE:NB * NE + NE], taken[:, :], ALU.add))
                dve.sem_inc(s_routed, 1)
                for c in range(2):
                    last = dve.tensor_tensor(oh[:, c, :, :], oh[:, c, :, :], pos_e[:, :, :], ALU.mult)
                link(last)
                dve.wait_ge(s_sent, b + 1)
                link(dve.tensor_reduce(pos_f[:, 0, :], oh[:, 0, :, :], AX.X, ALU.add))
                link(dve.tensor_reduce(pos_f[:, 1, :], oh[:, 1, :, :], AX.X, ALU.add))
                link(dve.tensor_copy(pos_i[:, :, :], pos_f[:, :, :]))
                link()
                dve.sem_inc(s_pos, 1)

            known_link = chain(s_cc, 1, 10 + 5 * (KNOWN // MAPPED))

            def place_tiles(link, memory, first, j0, start):
                ends = memory[:, 0:MAPPED * NE].rearrange("p (j e) -> p j e", e=NE)
                numbers = tile_no[:, first:first + MAPPED]
                link(dve.tensor_tensor(ends, over_t(upto[:, :], MAPPED), over_e(numbers, MAPPED), ALU.is_le))
                link(dve.tensor_reduce(tile_f[:, 0, :], ends, AX.X, ALU.add))
                link(dve.tensor_tensor(ends, ends, over_t(step[:, :], MAPPED), ALU.mult))
                link(dve.tensor_reduce(tile_f[:, 1, :], ends, AX.X, ALU.add))
                dve.tensor_scalar(tile_i[:, 0, j0:j0 + MAPPED], tile_f[:, 0, :], float(NE - 1), None, ALU.min)
                link(dve.scalar_tensor_tensor(out=tile_i[:, 1, j0:j0 + MAPPED], in0=tile_f[:, 1, :], scalar=start,
                                              in1=tile_row[:, first:first + MAPPED], op0=ALU.add, op1=ALU.add))

            def known_counts():
                link = known_link
                link(dve.tensor_tensor(count[:, :], taken[:, :], region[:, :], ALU.subtract))
                link(dve.tensor_copy(cnt_i[:, 0, :], count[:, :]))
                link(dve.tensor_scalar(cnt_i[:, 1, :], cnt_i[:, 0, :], P.bit_length() - 1, None, ALU.logical_shift_right))
                link(dve.tensor_copy(full[:, :], cnt_i[:, 1, :]))
                dve.memset(done_t[:, :], 0.0)
                link(dve.memset(one_e[:, :], 1.0))
                link(dve.tensor_tensor_scan(upto[:, :], one_e[:, :], full[:, :], 0.0, ALU.mult, ALU.add))
                link(dve.tensor_scalar(step[:, :], full[:, :], -float(P), float(REGION), ALU.mult, ALU.add))
                link(dve.tensor_tensor(done_t[:, 0:NE], full[:, :], upto[:, :], ALU.subtract))
                link(dve.tensor_scalar(done_t[:, 0:NE], done_t[:, 0:NE], float(KNOWN), 0.0, ALU.add, ALU.max))
                link(dve.tensor_tensor(done_t[:, 0:NE], done_t[:, 0:NE], full[:, :], ALU.min))
                dve.wait_ge(s_xt, NCHUNK - 1)
                dve.wait_ge(s_parts, NCHUNK)
                dve.wait_ge(s_feat, 16 * B)

            def known_tiles(n):
                place_tiles(known_link, xs[:, :, :].rearrange("p t c -> p (t c)"), MAPPED * n, MAPPED * n, 0.0)
                if MAPPED * (n + 1) == KNOWN:
                    known_link()
                    dve.sem_inc(s_map, 1)

            def rest_tiles():
                link = chain(s_cc, 1 + 10 + 5 * (KNOWN // MAPPED), 14)
                dve.tensor_copy(cnt_fill, taken[:, :]).then_inc(s_filled_at, 1)
                link(dve.tensor_tensor(count[:, :], taken[:, :], region[:, :], ALU.subtract))
                link(dve.tensor_scalar(cnt_i[:, 0, :], count[:, :], float(P - 1), None, ALU.add))
                link(dve.tensor_scalar(cnt_i[:, 1, :], cnt_i[:, 0, :], P.bit_length() - 1, None, ALU.logical_shift_right))
                link(dve.tensor_copy(all_t[:, :], cnt_i[:, 1, :]))
                link(dve.tensor_tensor(left_t[:, :], all_t[:, :], done_t[:, 0:NE], ALU.subtract))
                link(dve.tensor_tensor_scan(upto[:, :], one_e[:, :], left_t[:, :], 0.0, ALU.mult, ALU.add))
                link(dve.tensor_tensor(step[:, :], done_t[:, 1:NE + 1], all_t[:, :], ALU.subtract))
                link(dve.tensor_scalar(step[:, :], step[:, :], float(P), float(REGION), ALU.mult, ALU.add))
                link(dve.tensor_scalar(first_row[:, :], done_t[:, 0:1], float(P), None, ALU.mult))
                place_tiles(link, nr, 0, KNOWN, first_row[:, 0:1])
                link()
                dve.sem_inc(s_map, 1)

            def slots(k, b, h, prep, fin):
                fb = b if h else b - 1
                batch_of[0] = b + h
                for s in range(S):
                    if prep and s == 0:
                        for i in range(CT):
                            make_score(k + 1, i)
                    if prep and s == 1:
                        top_first(k + 1)
                    if fin and s == 2:
                        agg_merge(k - 1, 1 - h)
                    if prep and s == 2:
                        top_drop(k + 1, (0, 1))
                    if prep and s == 3:
                        top_drop(k + 1, (2, 3))
                    if fin and s == 4:
                        gnn_out(k - 1, fb, 1 - h)
                        ln2_stats(k - 1)
                    if fin and s == 5:
                        ln2_apply(k - 1, fb, 1 - h)
                    if s in REDUCED[h]:
                        near_reduce(k, b, h, REDUCED[h].index(s))
                    if prep and h and s == 6:
                        ln1_stats(k + 1, b + 1)
                    if prep and s == 6:
                        top_second(k + 1)
                    if prep and s == 7:
                        neighbour_rows(k + 1, 1 - h)
                    if prep and h and s == 8:
                        ln1_apply(k + 1, b + 1)
                    if fin and s == 8:
                        logits_out(k - 1, 1 - h)
                    if fin and h == 0 and s == 9:
                        route_first(fb)
                    if prep and h and s == 10:
                        lo_part(b + 1)
                    if prep and s == 11:
                        agg_init(k + 1, 1 - h)
                    if fin and h == 0 and s == 12:
                        route_second(fb)
                    if not prep and s == 6:
                        known_counts()
                    if not prep and s in (7, 8):
                        known_tiles(s - 7)
                    ahead = s + NRING - 1
                    if ahead < S:
                        make_onehot(k, h, ahead)
                    elif prep:
                        make_onehot(k + 1, 1 - h, ahead - S)
                    take_max(k, h, s)

            dve.sem_inc(s_lgd, 1)
            dve.sem_inc(s_routed, 1)
            dve.memset(feat_end[:, :], float(N - FEAT)).then_inc(s_fe, 1)
            dve.wait_ge(s_falling, 1)
            for i in range(CT):
                make_score(0, i)
            top_first(0)
            ln1_stats(0, 0)
            top_drop(0, range(CT))
            ln1_apply(0, 0)
            top_second(0)
            dve.wait_ge(s_fe, 1)
            neighbour_rows(0, 0)
            lo_part(0)
            agg_init(0, 0)
            for s in range(NRING - 1):
                make_onehot(0, 0, s)
            dve.wait_ge(s_const, N_CONST)
            dve.tensor_copy(taken[:, :], region[:, :]).then_inc(s_cc, 1)
            dve.wait_ge(s_cc, 1)
            chunks(dve, slots)
            agg_merge(NCHUNK - 1, 1)
            gnn_out(NCHUNK - 1, B - 1, 1)
            ln2_stats(NCHUNK - 1)
            ln2_apply(NCHUNK - 1, B - 1, 1)
            logits_out(NCHUNK - 1, 1)
            route_first(B - 1)
            route_second(B - 1)

            rest_tiles()

            kept = [dve.alloc_register(f"expert_of_tile{u}") for u in range(UN)]

            def load_expert(j, u):
                dve.load(kept[u % UN], tile_i[0:1, 0, ds(j, 1)])

            def copy_weights(j, u):
                e = dve.snap(kept[u % UN], min_val=0, max_val=NE - 1)
                wait(dve, s_h, j - 1)
                dve.tensor_copy(w_tile[:, u % 2, :], w12[:, ds(e, 1), :].rearrange("p a h -> p (a h)"))\
                    .then_inc(s_wt, 1)

            def hidden(j, u):
                dve.wait_ge(s_silu, j + 1)
                wait(dve, s_y, j - 1)
                dve.tensor_tensor(hid_t[:, u % 2, :], bank[2 + u % 2][:, HID:2 * HID], silu[:, u % 2, :], ALU.mult)\
                    .then_inc(s_hid, 1)

            def tiles(j0, turn, left):
                for u in range(UN):
                    if u + 1 < left:
                        hidden(j0 + u + 1, u + 1)
                    if u + 4 < left:
                        load_expert(j0 + u + 4, u + 4)
                    if u + 3 < left:
                        copy_weights(j0 + u + 3, u + 3)

            dve.wait_ge(s_wexp, 64)
            for u in range(4):
                load_expert(u, u)
            for u in range(3):
                if u == 2:
                    hidden(0, 0)
                copy_weights(u, u)
            expert_turns(dve, tiles)

            dve.wait_ge(s_exp, 1)
            dve.tensor_scalar(weight[:, 2, :], gap_exp[:, :], 1.0, None, ALU.add).then_inc(s_share, 1)
            dve.wait_ge(s_share, 1)
            dve.reciprocal(weight[:, 0, :], weight[:, 2, :]).then_inc(s_share, 1)
            dve.wait_ge(s_share, 2)
            dve.tensor_tensor(weight[:, 1, :], gap_exp[:, :], weight[:, 0, :], ALU.mult).then_inc(s_share, 1)
            dve.wait_ge(s_share, 3)
            for q in range(TILES // QT):
                g = q % GB
                dve.wait_ge(s_g[g], 16 * (q // GB + 1))
                if q >= GB:
                    dve.wait_ge(s_out[g], 16 * (q // GB))
                for i in range(QT):
                    t = q * QT + i
                    dve.scalar_tensor_tensor(out=res[:, g, i, :], in0=pairs_in[:, g, i, 0:C], scalar=weight[:, 0, t:t + 1],
                                             in1=x1[:, t, :], op0=ALU.mult, op1=ALU.add).then_inc(s_c1, 1)
                for i in range(QT):
                    t = q * QT + i
                    dve.wait_ge(s_c1, t + 1)
                    dve.scalar_tensor_tensor(out=res[:, g, i, :], in0=pairs_in[:, g, i, C:2 * C], scalar=weight[:, 1, t:t + 1],
                                             in1=res[:, g, i, :], op0=ALU.mult, op1=ALU.add).then_inc(s_res, 1)

        @block.tensor
        def _(pe):
            def transpose_score(k, q):
                pe.wait_ge(s_score, CT * (k + 1))
                wait(pe, s_tev, NPIECE * k + q)
                for c in range(PIECE):
                    j = PIECE * q + c
                    for i in range(CT):
                        last = pe.transpose(tr_ps[:, c, i * P:(i + 1) * P], score[:, i, j * P:(j + 1) * P], ident16[:, :])
                last.then_inc(s_tr, 1)

            def rank_product(k, n):
                j, r = n // 2 + NB // 2 * (n % 2), n % 2
                pe.wait_ge(s_tev, NPIECE * (k + 1))
                if n == 0:
                    wait(pe, s_rev, NB * k)
                elif n == 1:
                    wait(pe, s_init, k)
                else:
                    pe.wait_ge(s_rev, NB * k + n - 1)
                parts = [(ones, i) for i in range(j)] if n == 1 else [(rank_next, j - 1)] if n else []
                for i, (m, c) in enumerate(parts + [(rank_mat, j)]):
                    last = pe.matmul(rk_ps[r][:, :], m[:, :], mask_t[:, c, :], start=(n < 2 and i == 0),
                                     stop=True, skip_group_check=True)
                last.then_inc(s_rk, 1)

            def degree_product(k):
                pe.wait_ge(s_rev, NB * (k + 1))
                pe.matmul(rk_ps[1][:, :], rank_next[:, :], mask_t[:, NB - 1, :], start=False, stop=True,
                          skip_group_check=True).then_inc(s_rk, 1)

            def slot_product(k, h, s):
                if s == 0:
                    pe.wait_ge(s_parts, k + 1)
                if s in ACT_SLOTS:
                    pe.wait_ge(s_oha, act_count(k, s) + 1)
                else:
                    pe.wait_ge(s_oh, dve_count(k, s) + 1)
                wait(pe, s_max, S * k + s - NRING + 1)
                r, a = (S * h + s) % NRING, slot_start(h, s)
                for j in range(NB):
                    for part_ in range(2):
                        last = pe.matmul(bank[r][:, a:], xparts[:, h, j, part_, :], onehot[:, r, j * CH + a:(j + 1) * CH],
                                         start=(j == 0 and part_ == 0), stop=(j == NB - 1 and part_ == 1))
                last.then_inc(s_slot, 1)

            def transpose_xs(k, b, h):
                pe.wait_ge(s_lgd, k + 1)
                if h == 0:
                    pe.wait_ge(s_routed, b + 1)
                for i in range(CT):
                    last = pe.transpose(fin_ps[:, i * P:(i + 1) * P], (xs_2 if h else xs)[:, i, :], ident32[:, :])
                last.then_inc(s_xt, 1)

            def transpose_near(k):
                pe.wait_ge(s_xtev, k + 1)
                pe.wait_ge(s_red, CT * (k + 1))
                for i in range(CT):
                    last = pe.transpose(fin_ps[:, i * P:(i + 1) * P], near_max[:, i, :], ident32[:, :])
                last.then_inc(s_nt, 1)

            def gnn_product(k, h):
                pe.wait_ge(s_agg, k + 1)
                for i in range(CT):
                    pe.matmul(fin_ps[:, i * P:(i + 1) * P], xs_t[:, i * P:(i + 1) * P], w_gnn[:, 0, :], start=True, stop=False)
                    last = pe.matmul(fin_ps[:, i * P:(i + 1) * P], agg[:, h, i * P:(i + 1) * P], w_gnn[:, 1, :],
                                     start=False, stop=True)
                last.then_inc(s_fin, 1)

            def transpose_x2(k, h):
                pe.wait_ge(s_pay, k + 1)
                for i in range(CT):
                    last = pe.transpose(fin_ps[:, i * P:(i + 1) * P], pay[:, 0, h, i, 0:C], ident32[:, :])
                last.then_inc(s_x2t, 1)

            def logit_product(k):
                pe.wait_ge(s_x2tev, k + 1)
                for i in range(CT):
                    last = pe.matmul(fin_ps[:, i * NE:(i + 1) * NE], x2_t[:, i * P:(i + 1) * P], gw[:, :], start=True, stop=True)
                last.then_inc(s_lg, 1)

            def route_product(b):
                pe.wait_ge(s_sel, b + 1)
                pe.matmul(fin_ps[:, 0:NB * NE], tri[:, :], sel16[:, :, :].rearrange("p t e -> p (t e)"),
                          start=True, stop=False, skip_group_check=True)
                for t in range(NB - 1):
                    pe.matmul(fin_ps[:, (t + 1) * NE:NB * NE], ones[:, :],
                              sel16[:, t, :].unsqueeze(1).broadcast_to([P, NB - 1 - t, NE]),
                              start=False, stop=False, skip_group_check=True)
                for t in range(NB):
                    last = pe.matmul(fin_ps[:, NB * NE:NB * NE + NE], ones[:, :], sel16[:, t, :],
                                     start=False, stop=(t == NB - 1), skip_group_check=True)
                last.then_inc(s_route, 1)

            def slots(k, b, h, prep, fin):
                fb = b if h else b - 1
                for s in range(S):
                    if fin and s == 1:
                        transpose_xs(k - 1, fb, 1 - h)
                    if fin and s == 2:
                        transpose_near(k - 1)
                    if prep and 2 <= s < 2 + NPIECE:
                        transpose_score(k + 1, s - 2)
                    if fin and s == 4:
                        gnn_product(k - 1, 1 - h)
                    if prep and 6 <= s < 6 + NB // 2:
                        rank_product(k + 1, 2 * (s - 6))
                        rank_product(k + 1, 2 * (s - 6) + 1)
                    if prep and s == 6 + NB // 2:
                        degree_product(k + 1)
                    if fin and s == 7:
                        transpose_x2(k - 1, 1 - h)
                    if fin and s == 8:
                        logit_product(k - 1)
                    if fin and h == 0 and s == 11:
                        route_product(fb)
                    slot_product(k, h, s)

            pe.wait_ge(s_const, N_CONST)
            pe.wait_ge(s_w, 64)
            for q in range(NPIECE):
                transpose_score(0, q)
            for n in range(NB):
                rank_product(0, n)
            degree_product(0)
            chunks(pe, slots)
            transpose_xs(NCHUNK - 1, B - 1, 1)
            transpose_near(NCHUNK - 1)
            gnn_product(NCHUNK - 1, 1)
            transpose_x2(NCHUNK - 1, 1)
            logit_product(NCHUNK - 1)
            route_product(B - 1)

            def transpose_rows(j, u, turn):
                pe.wait_ge(s_xd[u % UN], 16 * (turn + 1 + u // UN))
                wait(pe, s_xdtev, j - 1)
                pe.transpose(bank[u % 2][:, 0:P], xd[:, u % UN, 0:C], ident32[:, :]).then_inc(s_xdt, 1)

            kept = [pe.alloc_register(f"expert_of_tile{u}") for u in range(UN)]

            def load_expert(j, u):
                pe.load(kept[u % UN], tile_i[0:1, 0, ds(j, 1)])

            def hidden_product(j, u):
                pe.wait_ge(s_xdtev, j + 1)
                pe.wait_ge(s_wt, j + 1)
                wait(pe, s_hid, j - 1)
                for c in range(4):
                    last = pe.matmul(bank[2 + u % 2][:, c * P:(c + 1) * P], w_tile[:, u % 2, c * P:(c + 1) * P],
                                     xd_t[:, u % 2, :], start=True, stop=True)
                last.then_inc(s_h, 1)

            def output_product(j, u):
                e = pe.snap(kept[u % UN], min_val=0, max_val=NE - 1)
                pe.wait_ge(s_hid, j + 1)
                wait(pe, s_yev, j - 1)
                for c in range(2):
                    last = pe.matmul(y_ps[u % 2][:, 0:P], hid_t[:, u % 2, c * P:(c + 1) * P],
                                     w3_sb[:, ds(e, 1), c, :].rearrange("p a o -> p (a o)"), start=(c == 0), stop=(c == 1))
                last.then_inc(s_y, 1)

            def tiles(j0, turn, left):
                for u in range(UN):
                    if u + 1 < left:
                        hidden_product(j0 + u + 1, u + 1)
                        load_expert(j0 + u + 1, u + 1)
                    if u or not isinstance(j0, int) or j0:
                        output_product(j0 + u - 1, u + UN - 1)
                    if u + 3 < left:
                        transpose_rows(j0 + u + 3, u + 3, turn)

            pe.wait_ge(s_map, 2)
            pe.wait_ge(s_wexp, 64)
            load_expert(0, 0)
            transpose_rows(0, 0, 0)
            transpose_rows(1, 1, 0)
            hidden_product(0, 0)
            transpose_rows(2, 2, 0)
            expert_turns(pe, tiles)
            output_product(PAIR_TILES - 1, UN - 1)


def kernel(**inputs):
    import numpy as _np
    import concourse.bacc as _bacc
    from concourse import mybir as _mybir
    from concourse.bass_utils import run_bass_kernel_spmd as _run

    names = ["x", "adj", "L0_gnn_W", "L0_gnn_b", "L0_ffn_gate_w", "L0_ffn_gate_b", "L0_ffn_w1", "L0_ffn_w2", "L0_ffn_w3"]
    nc = _bacc.Bacc("TRN2", target_bir_lowering=False, num_devices=1)
    arrays, args = {}, []
    for name in names:
        a = _np.ascontiguousarray(inputs[name])
        arrays[f"in_{name}"] = a
        args.append(nc.dram_tensor(f"in_{name}", a.shape, _mybir.dt.from_np(a.dtype), kind="ExternalInput").ap())
    shape = inputs["x"].shape
    args.append(nc.dram_tensor("out_0", shape, _mybir.dt.float32, kind="ExternalOutput").ap())
    build(nc, *args)
    r = _run(nc, [arrays], core_ids=[0])
    return r.results[0]["out_0"]
```
